# Optimizing a Trainium2 kernel written in Bass

```python
import numpy as np
import jax
import jax.numpy as jnp

def _softmax(x, axis=-1):
    return jax.nn.softmax(x, axis=axis)

def _gelu(x):
    return jax.nn.gelu(x, approximate=True)

def _silu(x):
    return jax.nn.silu(x)

def _sigmoid(x):
    return jax.nn.sigmoid(x)

def _layernorm(x, axis=-1, eps=1e-05):
    m = jnp.mean(x, axis=axis, keepdims=True)
    v = jnp.var(x, axis=axis, keepdims=True)
    return (x - m) / jnp.sqrt(v + eps)

def _scatter_add(tgt, idx, src, axis=0):
    return tgt.at[idx].add(src)

def _segment_sum(src, seg, n):
    return jax.ops.segment_sum(src, seg, n)
kernel_name = 'mk_conv_preact_d2_conv_nchw256_r4_c53013'

def setup_inputs(seed: int=0):
    np.random.seed(seed)
    _w = jnp.asarray

    def _rec_inputs():
        import jax
        import jax.numpy as jnp
        _gk = jax.random.key(seed)
        x = 1.648e-05 + 1 * jax.random.normal(jax.random.fold_in(_gk, 1), (4, 64, 24, 24), jnp.float32)
        return x
    x = _rec_inputs()

    def _L0_conv_setup():
        import jax, jax.numpy as jnp
        import numpy as np
        K = 3
        PAD = 1
        STRIDE = 1

        def _deform_conv_layer(x, w_off, b_off, w_def, b_def):
            B, C, H, W = x.shape
            K2 = K * K
            offset = jax.lax.conv_general_dilated(x, w_off, window_strides=(STRIDE, STRIDE), padding=[(PAD, PAD), (PAD, PAD)], dimension_numbers=('NCHW', 'OIHW', 'NCHW')) + b_off[None, :, None, None]
            Ho, Wo = (offset.shape[2], offset.shape[3])
            off = offset.reshape(B, K2, 2, Ho, Wo)
            off_y, off_x = (off[:, :, 0], off[:, :, 1])
            ky, kx = jnp.meshgrid(jnp.arange(K), jnp.arange(K), indexing='ij')
            ky = ky.reshape(K2).astype(x.dtype)
            kx = kx.reshape(K2).astype(x.dtype)
            base_y = (jnp.arange(Ho) * STRIDE - PAD).astype(x.dtype)
            base_x = (jnp.arange(Wo) * STRIDE - PAD).astype(x.dtype)
            py = base_y[None, None, :, None] + ky[None, :, None, None] + off_y
            px = base_x[None, None, None, :] + kx[None, :, None, None] + off_x
            y0f = jnp.floor(py)
            x0f = jnp.floor(px)
            wy1 = py - y0f
            wy0 = 1.0 - wy1
            wx1 = px - x0f
            wx0 = 1.0 - wx1
            y0 = y0f.astype(jnp.int32)
            x0 = x0f.astype(jnp.int32)
            xf = x.reshape(B, C, H * W)

            def corner(yi, xi, wgt):
                valid = ((yi >= 0) & (yi < H) & (xi >= 0) & (xi < W)).astype(x.dtype)
                idx = jnp.clip(yi, 0, H - 1) * W + jnp.clip(xi, 0, W - 1)
                g = jnp.take_along_axis(xf, idx.reshape(B, 1, -1), axis=2)
                g = g.reshape(B, C, K2, Ho, Wo)
                return g * (wgt * valid).reshape(B, 1, K2, Ho, Wo)
            val = corner(y0, x0, wy0 * wx0) + corner(y0, x0 + 1, wy0 * wx1) + corner(y0 + 1, x0, wy1 * wx0) + corner(y0 + 1, x0 + 1, wy1 * wx1)
            out = jnp.einsum('bckhw,ock->bohw', val, w_def.reshape(-1, C, K2))
            return out + b_def[None, :, None, None]
        key = jax.random.key(seed)
        k0, k1, k2, k3 = jax.random.split(key, 4)
        B, Cin, Cout, H, W = (4, 64, 64, 24, 24)
        K2 = K * K
        x = jax.random.normal(k0, (B, Cin, H, W), jnp.float32)
        w_off = jax.random.normal(k1, (2 * K2, Cin, K, K), jnp.float32) * 0.01
        b_off = jnp.zeros((2 * K2,), jnp.float32)
        w_def = jax.random.normal(k2, (Cout, Cin, K, K), jnp.float32) * (1.0 / np.sqrt(Cin * K2))
        b_def = jax.random.normal(k3, (Cout,), jnp.float32) * 0.01
        return {'x': x, 'w_off': w_off, 'b_off': b_off, 'w_def': w_def, 'b_def': b_def}
    _L0_conv_all = _L0_conv_setup()
    _L0_conv_in = {k: v for k, v in _L0_conv_all.items() if k in ('w_off', 'b_off', 'w_def', 'b_def')}
    del _L0_conv_all

    def _L1_conv_setup():
        import jax, jax.numpy as jnp
        import numpy as np
        K = 3
        PAD = 1
        STRIDE = 1
        DIL = 1
        GN_EPS = 1e-05

        def _conv2d(x, w, b):
            y = jax.lax.conv_general_dilated(x, w, (STRIDE, STRIDE), [(PAD, PAD), (PAD, PAD)], rhs_dilation=(DIL, DIL), dimension_numbers=('NCHW', 'OIHW', 'NCHW'))
            return y + b[None, :, None, None]

        def _modulated_deform_conv(x, w_off, b_off, w, b):
            B, C, H, W = x.shape
            KK = K * K
            off = _conv2d(x, w_off, b_off)
            o1, o2, m = jnp.split(off, 3, axis=1)
            offset = jnp.concatenate([o1, o2], axis=1)
            mask = jax.nn.sigmoid(m)
            offset = offset.reshape(B, KK, 2, H, W)
            dy, dx = (offset[:, :, 0], offset[:, :, 1])
            ki = jnp.arange(KK) // K
            kj = jnp.arange(KK) % K
            base_y = jnp.arange(H)[None, :, None] - PAD + ki[:, None, None] * DIL
            base_x = jnp.arange(W)[None, None, :] - PAD + kj[:, None, None] * DIL
            py = base_y.astype(x.dtype) + dy
            px = base_x.astype(x.dtype) + dx
            y0f = jnp.floor(py)
            x0f = jnp.floor(px)
            ly = py - y0f
            lx = px - x0f
            y0 = y0f.astype(jnp.int32)
            x0 = x0f.astype(jnp.int32)
            xf = x.reshape(B, C, H * W)

            def gather(yi, xi):
                valid = (yi >= 0) & (yi < H) & (xi >= 0) & (xi < W)
                idx = jnp.clip(yi, 0, H - 1) * W + jnp.clip(xi, 0, W - 1)
                g = jax.vmap(lambda xb, ib: jnp.take(xb, ib.reshape(-1), axis=1))(xf, idx)
                g = g.reshape(B, C, KK, H, W)
                return g * valid[:, None].astype(x.dtype)
            val = gather(y0, x0) * ((1 - ly) * (1 - lx))[:, None] + gather(y0, x0 + 1) * ((1 - ly) * lx)[:, None] + gather(y0 + 1, x0) * (ly * (1 - lx))[:, None] + gather(y0 + 1, x0 + 1) * (ly * lx)[:, None]
            val = val * mask[:, None]
            out = jnp.einsum('bckhw,ock->bohw', val, w.reshape(w.shape[0], C, KK))
            return out + b[None, :, None, None]

        def _groupnorm1_relu(y, gamma, beta):
            mu = y.mean(axis=(1, 2, 3), keepdims=True)
            var = y.var(axis=(1, 2, 3), keepdims=True)
            yn = (y - mu) * jax.lax.rsqrt(var + GN_EPS)
            return jax.nn.relu(yn * gamma[None, :, None, None] + beta[None, :, None, None])
        key = jax.random.key(seed)
        ks = jax.random.split(key, 5)
        B, C, H, W = (4, 64, 16, 16)
        CO = 64
        x = jax.random.normal(ks[0], (B, C, H, W), jnp.float32)
        w_off = jax.random.normal(ks[1], (3 * K * K, C, K, K), jnp.float32) * 0.01
        b_off = jax.random.normal(ks[2], (3 * K * K,), jnp.float32) * 0.01
        w = jax.random.normal(ks[3], (CO, C, K, K), jnp.float32) * (1.0 / np.sqrt(C * K * K))
        b = jax.random.normal(ks[4], (CO,), jnp.float32) * 0.01
        gamma = jnp.ones((CO,), jnp.float32)
        beta = jnp.zeros((CO,), jnp.float32)
        return dict(x=x, w_off=w_off, b_off=b_off, w=w, b=b, gamma=gamma, beta=beta)
    _L1_conv_all = _L1_conv_setup()
    _L1_conv_in = {k: v for k, v in _L1_conv_all.items() if k in ('w_off', 'b_off', 'w', 'b', 'gamma', 'beta')}
    del _L1_conv_all
    return {'x': x, 'L0_conv_w_off': _L0_conv_in['w_off'], 'L0_conv_b_off': _L0_conv_in['b_off'], 'L0_conv_w_def': _L0_conv_in['w_def'], 'L0_conv_b_def': _L0_conv_in['b_def'], 'L1_conv_w_off': _L1_conv_in['w_off'], 'L1_conv_b_off': _L1_conv_in['b_off'], 'L1_conv_w': _L1_conv_in['w'], 'L1_conv_b': _L1_conv_in['b'], 'L1_conv_gamma': _L1_conv_in['gamma'], 'L1_conv_beta': _L1_conv_in['beta']}

def reference(x, L0_conv_w_off, L0_conv_b_off, L0_conv_w_def, L0_conv_b_def, L1_conv_w_off, L1_conv_b_off, L1_conv_w, L1_conv_b, L1_conv_gamma, L1_conv_beta):
    import jax
    import jax.numpy as jnp

    def _L0_conv_ref(x, w_off, b_off, w_def, b_def):
        import jax, jax.numpy as jnp
        import numpy as np
        K = 3
        PAD = 1
        STRIDE = 1

        def _deform_conv_layer(x, w_off, b_off, w_def, b_def):
            B, C, H, W = x.shape
            K2 = K * K
            offset = jax.lax.conv_general_dilated(x, w_off, window_strides=(STRIDE, STRIDE), padding=[(PAD, PAD), (PAD, PAD)], dimension_numbers=('NCHW', 'OIHW', 'NCHW')) + b_off[None, :, None, None]
            Ho, Wo = (offset.shape[2], offset.shape[3])
            off = offset.reshape(B, K2, 2, Ho, Wo)
            off_y, off_x = (off[:, :, 0], off[:, :, 1])
            ky, kx = jnp.meshgrid(jnp.arange(K), jnp.arange(K), indexing='ij')
            ky = ky.reshape(K2).astype(x.dtype)
            kx = kx.reshape(K2).astype(x.dtype)
            base_y = (jnp.arange(Ho) * STRIDE - PAD).astype(x.dtype)
            base_x = (jnp.arange(Wo) * STRIDE - PAD).astype(x.dtype)
            py = base_y[None, None, :, None] + ky[None, :, None, None] + off_y
            px = base_x[None, None, None, :] + kx[None, :, None, None] + off_x
            y0f = jnp.floor(py)
            x0f = jnp.floor(px)
            wy1 = py - y0f
            wy0 = 1.0 - wy1
            wx1 = px - x0f
            wx0 = 1.0 - wx1
            y0 = y0f.astype(jnp.int32)
            x0 = x0f.astype(jnp.int32)
            xf = x.reshape(B, C, H * W)

            def corner(yi, xi, wgt):
                valid = ((yi >= 0) & (yi < H) & (xi >= 0) & (xi < W)).astype(x.dtype)
                idx = jnp.clip(yi, 0, H - 1) * W + jnp.clip(xi, 0, W - 1)
                g = jnp.take_along_axis(xf, idx.reshape(B, 1, -1), axis=2)
                g = g.reshape(B, C, K2, Ho, Wo)
                return g * (wgt * valid).reshape(B, 1, K2, Ho, Wo)
            val = corner(y0, x0, wy0 * wx0) + corner(y0, x0 + 1, wy0 * wx1) + corner(y0 + 1, x0, wy1 * wx0) + corner(y0 + 1, x0 + 1, wy1 * wx1)
            out = jnp.einsum('bckhw,ock->bohw', val, w_def.reshape(-1, C, K2))
            return out + b_def[None, :, None, None]
        return _deform_conv_layer(x, w_off, b_off, w_def, b_def)

    def _L1_conv_ref(x, w_off, b_off, w, b, gamma, beta):
        import jax, jax.numpy as jnp
        import numpy as np
        K = 3
        PAD = 1
        STRIDE = 1
        DIL = 1
        GN_EPS = 1e-05

        def _conv2d(x, w, b):
            y = jax.lax.conv_general_dilated(x, w, (STRIDE, STRIDE), [(PAD, PAD), (PAD, PAD)], rhs_dilation=(DIL, DIL), dimension_numbers=('NCHW', 'OIHW', 'NCHW'))
            return y + b[None, :, None, None]

        def _modulated_deform_conv(x, w_off, b_off, w, b):
            B, C, H, W = x.shape
            KK = K * K
            off = _conv2d(x, w_off, b_off)
            o1, o2, m = jnp.split(off, 3, axis=1)
            offset = jnp.concatenate([o1, o2], axis=1)
            mask = jax.nn.sigmoid(m)
            offset = offset.reshape(B, KK, 2, H, W)
            dy, dx = (offset[:, :, 0], offset[:, :, 1])
            ki = jnp.arange(KK) // K
            kj = jnp.arange(KK) % K
            base_y = jnp.arange(H)[None, :, None] - PAD + ki[:, None, None] * DIL
            base_x = jnp.arange(W)[None, None, :] - PAD + kj[:, None, None] * DIL
            py = base_y.astype(x.dtype) + dy
            px = base_x.astype(x.dtype) + dx
            y0f = jnp.floor(py)
            x0f = jnp.floor(px)
            ly = py - y0f
            lx = px - x0f
            y0 = y0f.astype(jnp.int32)
            x0 = x0f.astype(jnp.int32)
            xf = x.reshape(B, C, H * W)

            def gather(yi, xi):
                valid = (yi >= 0) & (yi < H) & (xi >= 0) & (xi < W)
                idx = jnp.clip(yi, 0, H - 1) * W + jnp.clip(xi, 0, W - 1)
                g = jax.vmap(lambda xb, ib: jnp.take(xb, ib.reshape(-1), axis=1))(xf, idx)
                g = g.reshape(B, C, KK, H, W)
                return g * valid[:, None].astype(x.dtype)
            val = gather(y0, x0) * ((1 - ly) * (1 - lx))[:, None] + gather(y0, x0 + 1) * ((1 - ly) * lx)[:, None] + gather(y0 + 1, x0) * (ly * (1 - lx))[:, None] + gather(y0 + 1, x0 + 1) * (ly * lx)[:, None]
            val = val * mask[:, None]
            out = jnp.einsum('bckhw,ock->bohw', val, w.reshape(w.shape[0], C, KK))
            return out + b[None, :, None, None]

        def _groupnorm1_relu(y, gamma, beta):
            mu = y.mean(axis=(1, 2, 3), keepdims=True)
            var = y.var(axis=(1, 2, 3), keepdims=True)
            yn = (y - mu) * jax.lax.rsqrt(var + GN_EPS)
            return jax.nn.relu(yn * gamma[None, :, None, None] + beta[None, :, None, None])
        y = _modulated_deform_conv(x, w_off, b_off, w, b)
        return _groupnorm1_relu(y, gamma, beta)

    def _gn(v, G=32, eps=1e-05):
        B_, C_, H_, W_ = v.shape
        g = v.reshape(B_, G, C_ // G, H_, W_)
        m = jnp.mean(g, axis=(2, 3, 4), keepdims=True)
        s = jnp.var(g, axis=(2, 3, 4), keepdims=True)
        return ((g - m) / jnp.sqrt(s + eps)).reshape(v.shape)

    def _ln_c(v, eps=1e-06):
        m = jnp.mean(v, axis=1, keepdims=True)
        s = jnp.var(v, axis=1, keepdims=True)
        return (v - m) / jnp.sqrt(s + eps)

    def _ln_t(v, eps=1e-05):
        m = jnp.mean(v, axis=-1, keepdims=True)
        s = jnp.var(v, axis=-1, keepdims=True)
        return (v - m) / jnp.sqrt(s + eps)

    def _to_tokens(v):
        B_, C_, H_, W_ = v.shape
        return v.reshape(B_, C_, H_ * W_).transpose(0, 2, 1)

    def _from_tokens(t, like):
        B_, C_, H_, W_ = like.shape
        return t.transpose(0, 2, 1).reshape(B_, C_, H_, W_)
    x = x + _L0_conv_ref(_gn(x), L0_conv_w_off, L0_conv_b_off, L0_conv_w_def, L0_conv_b_def)
    x = x + _L1_conv_ref(_gn(x), L1_conv_w_off, L1_conv_b_off, L1_conv_w, L1_conv_b, L1_conv_gamma, L1_conv_beta)
    return x

_drawn_inputs = setup_inputs


def setup_inputs(seed=0):
    import zlib

    import numpy as np

    out = dict(_drawn_inputs(seed))
    spreads = {'L0_conv_b_off': (0.0, 0.1), 'L1_conv_gamma': (1.0, 0.2), 'L1_conv_beta': (0.0, 0.1)}
    factors = {'L0_conv_b_def': 6.183, 'L1_conv_b_off': 7.09, 'L1_conv_b': 4.492}
    for name, (base, spread) in spreads.items():
        noise = np.random.default_rng([zlib.crc32(name.encode()), seed]).standard_normal(out[name].shape)
        drawn = base * np.exp(spread * noise) if base else spread * noise
        out[name] = jnp.asarray(drawn.astype(out[name].dtype))
    for name, factor in factors.items():
        out[name] = (out[name] * factor).astype(out[name].dtype)
    return out
```

```python
from contextlib import ExitStack

import numpy as np

import concourse.bass as bass
from concourse import mybir

F32, F16, I32 = mybir.dt.float32, mybir.dt.float16, mybir.dt.int32
ALU = mybir.AluOpType
ACT = mybir.ActivationFunctionType
AX = mybir.AxisListType

B, C, H, W = 4, 64, 24, 24
HW = H * W
TAPS = 9
LAYERS = 2
PAIRS = B // 2
HALF = HW // 2
PADW = W + 2
BANK = 512

ROWS = 5
CHUNKS = -(-H // ROWS)
REACH = 2
BIG = 32.0
OFF = 27
NOFF = 2 * TAPS
LO = 32
KPOS = 67
KMASK = LO + OFF
YROWS = 2 * TAPS * ROWS
GN_EPS = 1e-5


def pixels(j):
    return W * (min(H, ROWS * (j + 1)) - ROWS * j)


def band(j, ky):
    a, b = ROWS * j, min(H, ROWS * (j + 1)) - 1
    return max(0, a - REACH - (ky - 1)), min(H, b + REACH - (ky - 1) + 1)


def wide(j):
    return min(band(j, ky)[0] for ky in range(3)), max(band(j, ky)[1] for ky in range(3))


WIDE_AT = [sum(wide(i)[1] - wide(i)[0] for i in range(j)) * W for j in range(CHUNKS + 1)]
WIDEST = max(wide(j)[1] - wide(j)[0] for j in range(CHUNKS)) * W
BANDEST = max(band(j, ky)[1] - band(j, ky)[0] for j in range(CHUNKS) for ky in range(3)) * W
SLOT = 256
TXCHUNK = 384
assert BANDEST <= SLOT and WIDEST <= BANK and 2 * HW == 3 * TXCHUNK

STEPS = [(p, ky, j) for p in range(PAIRS) for ky in range(3) for j in range(CHUNKS)]
ITEMS = 2 * len(STEPS)
UNIT_ITEMS = 2 * CHUNKS
TX_SLOTS, S_SLOTS = 2, 4

T_WT, T_Z, T_Y, T_MAIN = 0, 2, 2 + B * CHUNKS, 2 + B * CHUNKS + PAIRS * CHUNKS
T_LAYER = T_MAIN + ITEMS


def x_jobs():
    jobs = {}
    for l in range(LAYERS):
        names = [(l, "norm")]
        if l:
            names += [(l, "mask", p, j, bb) for p in range(PAIRS) for j in range(CHUNKS) for bb in range(2)]
        names += [(l, "flag")]
        names += [(l, "tx", u, kx, c) for u in range(3 * PAIRS) for kx in range(3) for c in range(3)]
        for n in names:
            jobs[n] = len(jobs)
    jobs["final mean"] = len(jobs)
    jobs["final var"] = len(jobs)
    return jobs


XJ = x_jobs()


def constants():
    q_row, q_col = np.arange(ROWS * W) // W, np.arange(ROWS * W) % W
    ex = np.zeros((128, TAPS, ROWS * W), np.float16)
    ef = np.zeros((128, TAPS, ROWS * W), np.float16)
    em = np.zeros((128, TAPS, ROWS * W), np.float16)
    for k in range(TAPS):
        ex[[2 * k + 1, LO + 2 * k + 1, 65], k] = 1
        ex[66, k] = k % 3 - 1 - q_col
        ef[[2 * k, LO + 2 * k, 64], k] = 1
        ef[66, k] = k // 3 - 1 - q_row
        em[[NOFF + k, LO + NOFF + k], k] = 1
    ey = np.zeros((128, CHUNKS, 2, TAPS, ROWS), np.float16)
    my = np.zeros((128, 2, TAPS, ROWS), np.float16)
    sel = np.zeros((128, TAPS, ROWS * W), np.float16)
    for k in range(TAPS):
        ey[[2 * k, LO + 2 * k, 64], :, :, k] = 1
        for j in range(CHUNKS):
            ey[66, j, :, k] = k // 3 - 1 - (ROWS * j + np.arange(ROWS))
        my[[NOFF + k, LO + NOFF + k], :, k] = 1
        for part in range(2):
            for i in range(ROWS):
                sel[(part * TAPS + k) * ROWS + i, k, q_row == i] = 1
    half = np.concatenate([a.reshape(128, -1) for a in (ex, ey, my, sel, ef, em)], 1)
    at = np.arange(128)
    same = at[:, None] // 2 == at[None, :] // 2
    ident = np.eye(128, dtype=np.float32)
    pair = np.where(same, 0.5, 0).astype(np.float32)
    diff = np.where(same, -0.5, 0).astype(np.float32) + ident
    block = np.where(at[:, None] // C == at[None, :] // C, 1 / C, 0).astype(np.float32)
    low = np.stack([at >= C, at >= TAPS * ROWS], 1) * np.float32(-1)
    rows = np.tile(-ROWS * np.arange(CHUNKS, dtype=np.float32), (128, 1))
    full = np.concatenate([ident, pair, diff, block, low, rows], 1)
    p = np.arange(HW)
    pos = np.stack([p // W, p % W, np.ones(HW)]).astype(np.float16)
    return half, full, np.repeat(pos[:, None], B, 1)


NHALF = TAPS * ROWS * W
HALF_AT = np.cumsum([0, NHALF, CHUNKS * YROWS, YROWS, NHALF, NHALF, NHALF])


def build(nc, x, w_off, w_def, vecs, c_half, c_full, c_pos, out):
    ctx = ExitStack()
    with ctx:
        def sb(name, shape, dt=F32):
            return ctx.enter_context(nc.sbuf_tensor(name, shape, dt))

        def sem(name):
            return ctx.enter_context(nc.semaphore(name))

        x_l = sb("x_l", [128, B, HW])
        xn = sb("xn", [128, B, HW])
        xh = sb("xh", [128, B, HW], F16)
        xpad = sb("xpad", [128, B, PADW * PADW], F16)
        xpad_v = xpad[:, :, :].rearrange("p b (h w) -> p b h w", h=PADW)
        w_raw = [[sb(f"w_raw{l}{i}", [128, TAPS * C]) for i in range(2)] for l in range(LAYERS)]
        w_unit = [sb(f"w_unit{i}", [128, TAPS, 2, C]) for i in range(2)]
        w_max = sb("w_max", [128, 2 * LAYERS])
        w_inv = sb("w_inv", [128, 2 * LAYERS])
        w_neg = sb("w_neg", [128, LAYERS])
        w_off16 = sb("w_off16", [128, TAPS, 64], F16)
        w_hi = sb("w_hi", [128, TAPS * C], F16)
        w_lo = sb("w_lo", [128, TAPS * C], F16)
        vec = sb("vec", [128, 6])
        half = sb("half", [128, int(HALF_AT[-1])], F16)
        full = sb("full", [128, 4 * 128 + 2 + CHUNKS])
        bn = sb("bn", [128, B, 2, 6])
        chan = sb("chan", [128, 2, B])
        group = sb("group", [128, 3, B])
        gsq = sb("gsq", [128, B])
        gvar = sb("gvar", [128, B])
        rstd = sb("rstd", [128, B])
        minus_half = sb("minus_half", [128, B])
        off_a = sb("off_a", [OFF, B, HW])
        off_b = sb("off_b", [OFF, B, HW])
        pos = sb("pos", [128, B, HW], F16)
        msk = sb("msk", [128, B, HW], F16)
        omax = sb("omax", [128, B])
        omax1 = sb("omax1", [128, 1])
        oall = sb("oall", [1, 1])
        flag = sb("flag", [1, LAYERS], I32)
        ya = sb("ya", [YROWS, 2, 2, WIDEST])
        yt = sb("yt", [YROWS, 2, 2, WIDEST])
        ym = sb("ym", [YROWS, 2, 2, WIDEST])
        yh = sb("yh", [YROWS, 2, 2, WIDEST], F16)
        ytent = sb("ytent", [YROWS, B, WIDE_AT[-1]], F16)
        z = sb("z", [ROWS * W, B, CHUNKS, TAPS * C])
        tx = sb("tx", [ROWS * W, TX_SLOTS, 3, 2 * HW])
        s = sb("s", [ROWS * W, S_SLOTS, 3, BANDEST])
        zeros = sb("zeros", [1, HALF], F16)
        y = sb("y", [128, PAIRS, HW])
        fin = sb("fin", [128, 8, PAIRS])
        res = sb("res", [128, PAIRS, HW])

        g_pos, g_msk = sb("g_pos", [KPOS, HW], F16), sb("g_msk", [KMASK, HW], F16)
        g_ex, g_ef, g_em = (sb(f"g_e{i}", [128, ROWS * W], F16) for i in range(3))
        g_xt, g_yt, g_s, g_z = tx[:, 0, 0, 0:HW], tx[:, 0, 1, 0:HW], tx[:, 0, 2, 0:HW], tx[:, 1, 0, 0:CHUNKS * C]

        def h(i, shape):
            v = half[:, int(HALF_AT[i]):int(HALF_AT[i + 1])]
            return v.rearrange("p (a b) -> p a b", a=shape)
        ex, ey, my, sel = h(0, TAPS), h(1, CHUNKS), h(2, 1), h(3, TAPS)
        ef, em = h(4, TAPS), h(5, TAPS)
        ident, pair_m, diff_m, block_m = (full[:, 128 * i:128 * (i + 1)] for i in range(4))
        low_c, low_y = full[:, 512:513], full[0:YROWS, 513:514]

        tb = ctx.enter_context(nc.psum_tensor("tb", [128, 2, 2 * BANK], F32))
        xb = ctx.enter_context(nc.psum_tensor("xb", [128, 2, BANK], F32))
        acc = ctx.enter_context(nc.psum_tensor("acc", [128, 2, BANK], F32))

        x_here = [sem(f"x_here{b}") for b in range(B)]
        w_here = [[sem(f"w_here{l}{i}") for i in range(2)] for l in range(LAYERS)]
        vec_here, half_here, full_here = sem("vec_here"), sem("half_here"), sem("full_here")
        pos_here = sem("pos_here")
        cleared = sem("cleared")
        t_full = [sem(f"t_full{i}") for i in range(2)]
        t_free = [sem(f"t_free{i}") for i in range(2)]
        xb_full = [sem(f"xb_full{i}") for i in range(2)]
        xb_free = [sem(f"xb_free{i}") for i in range(2)]
        acc_full, acc_free = sem("acc_full"), sem("acc_free")
        w_scaled = sem("w_scaled")
        wt_high = sem("wt_high")
        wt_done = sem("wt_done")
        dve_c = sem("dve_c")
        act_c = sem("act_c")
        stats_ready, gvar_ready, rstd_ready = sem("stats_ready"), sem("gvar_ready"), sem("rstd_ready")
        xn_ready, xh_ready, x16_ready = sem("xn_ready"), sem("xh_ready"), sem("x16_ready")
        xpad_ready = sem("xpad_ready")
        off_parts = sem("off_parts")
        off_sum = sem("off_sum")
        pos_high, pos_ready = sem("pos_high"), sem("pos_ready")
        sig_ready, msk_high, msk_ready = sem("sig_ready"), sem("msk_high"), sem("msk_ready")
        omax_ready = sem("omax_ready")
        yt_ready, ym_ready, yh_ready, ytent_ready = sem("yt_ready"), sem("ym_ready"), sem("yh_ready"), sem("ytent_ready")
        z_ready = sem("z_ready")
        tx_abs, tx_ready = sem("tx_abs"), sem("tx_ready")
        s_ready, s_used = sem("s_ready"), sem("s_used")
        y_ready = sem("y_ready")
        flag_ready = sem("flag_ready")
        x_mid_ready = sem("x_mid_ready")
        fin_ready, relu_ready, res_ready = sem("fin_ready"), sem("relu_ready"), sem("res_ready")
        fin_in = sem("fin_in")
        stored = sem("stored")
        g_act, g_dve, g_pe, g_sum, g_out = ([sem(f"{n}{l}") for l in range(LAYERS)]
                                            for n in ("g_act", "g_dve", "g_pe", "g_sum", "g_out"))

        block = ctx.enter_context(nc.Block())

        def tbuf(n):
            return tb[:, n % 2, :]

        def g_steps(l):
            return 7 + 2 * l + CHUNKS, CHUNKS * (2 + l), 1 + 2 * CHUNKS

        def halves(v):
            return v.rearrange("p (h c) -> p h c", h=2)

        def g_flag(eng, l):
            eng.wait_ge(flag_ready, l + 1)
            return eng.value_load(flag[0:1, l:l + 1], min_val=0, max_val=1)

        @block.sync
        def _(sp):
            for b in range(B):
                for d in range(2):
                    sp.dma_start(x_l[64 * d:64 * d + 64, b, :], x[b]).then_inc(x_here[b], 16)
                if b == 0:
                    sp.dma_start(full[:, :], c_full).then_inc(full_here, 16)
            sp.dma_start(w_raw[1][0][:, :], w_off[1]).then_inc(w_here[1][0], 16)
            sp.dma_start(w_raw[1][1][:, :], w_def[1]).then_inc(w_here[1][1], 16)
            sp.wait_ge(cleared, 3)
            sp.dma_start(pos[64:KPOS, :, :], c_pos).then_inc(pos_here, 16)
            for p in range(PAIRS):
                sp.wait_ge(res_ready, 2 * p + 2)
                for bb in range(2):
                    sp.dma_start(out[2 * p + bb], res[64 * bb:64 * bb + 64, p, :]).then_inc(stored, 16)
            sp.wait_ge(stored, 16 * B)

        @block.gpsimd
        def _(pool):
            nc.gpsimd.memset(xpad[:, :, :], 0.0).then_inc(cleared, 1)
            nc.gpsimd.memset(zeros[:, :], 0.0).then_inc(cleared, 1)
            nc.gpsimd.memset(pos[:, :, :], 0.0).then_inc(cleared, 1)
            nc.gpsimd.memset(msk[:, :, :], 0.0).then_inc(cleared, 1)
            nc.gpsimd.memset(minus_half[:, :], -0.5).then_inc(cleared, 1)
            pool.wait_ge(cleared, 5)
            for l in range(LAYERS):
                pool.wait_ge(gvar_ready, l + 1)
                nc.gpsimd.tensor_tensor(rstd[:, :], gvar[:, :], minus_half[:, :], ALU.pow).then_inc(rstd_ready, 1)
                for b in range(B):
                    if l:
                        pool.wait_ge(acc_full, 4 * l - 2)
                    pool.wait_ge(x16_ready, B * l + b + 1)
                    nc.gpsimd.tensor_copy(xpad_v[:, b, 1:H + 1, 1:W + 1],
                                          xh[:, b, :].rearrange("p (h w) -> p h w", h=H)).then_inc(xpad_ready, 1)
                for u in range(3 * PAIRS):
                    for kx in range(3):
                        n = (l * 3 * PAIRS + u) * 3 + kx
                        pool.wait_ge(tx_abs, 3 * (n + 1))
                        v = tx[:, u % TX_SLOTS, kx, :]
                        nc.gpsimd.tensor_scalar(v, v, 1.0, 0.0, ALU.min, ALU.max).then_inc(tx_ready, 1)
            pool.wait_ge(fin_in, 1)
            nc.gpsimd.tensor_tensor(fin[:, 5, :], fin[:, 4, :], minus_half[:, 0:PAIRS], ALU.pow)\
                .then_inc(rstd_ready, 1)

        @block.scalar
        def _(act):
            act.dma_start(w_raw[0][0][:, :], w_off[0]).then_inc(w_here[0][0], 16)
            act.dma_start(vec[:, :], vecs).then_inc(vec_here, 16)
            act.dma_start(w_raw[0][1][:, :], w_def[0]).then_inc(w_here[0][1], 16)
            act.dma_start(half[:, :], c_half).then_inc(half_here, 16)

            def weights(l):
                n = T_LAYER * l + T_WT
                act.wait_ge(t_full[n % 2], n // 2 + 1)
                if l:
                    act.wait_ge(acc_full, 4 * l)
                    act.wait_ge(t_full[1], (T_LAYER * l + T_Z) // 2)
                nc.scalar.activation(w_off16[:, :, 0:32],
                                     tbuf(n)[:, 0:TAPS * 64].rearrange("p (t o) -> p t o", t=TAPS)[:, :, 0:32],
                                     ACT.Copy).then_inc(wt_high, 1)
                n += 1
                act.wait_ge(t_full[n % 2], n // 2 + 1)
                nc.scalar.activation(w_hi[:, :], tbuf(n)[:, 0:TAPS * C], ACT.Copy).then_inc(wt_high, 1)

            def split_x(l):
                for b in range(B):
                    act.wait_ge(xn_ready, B * l + b + 1)
                    if l:
                        act.wait_ge(z_ready, B * CHUNKS)
                        act.wait_ge(xpad_ready, B)
                    nc.scalar.activation(xh[:, b, :], xn[:, b, :], ACT.Copy).then_inc(xh_ready, 1)

            def offsets(l, p):
                act.wait_ge(acc_full, 4 * l + p + 1)
                v = acc[:, :, 0:HALF]
                for bb in range(2):
                    b = 2 * p + bb
                    if l:
                        act.wait_ge(omax_ready, B + 1)
                        act.wait_ge(pos_ready, B)
                    for i, dst in enumerate((off_a, off_b)):
                        r = slice(64 * bb + LO * i, 64 * bb + LO * i + OFF)
                        last = nc.scalar.activation(
                            dst[:, b, :].rearrange("o (h c) -> o h c", h=2), v[r], ACT.Identity,
                            scale=w_max[r, 2 * l:2 * l + 1], bias=vec[r, l:l + 1] if i == 0 else 0.0)
                        last.then_inc(off_parts, 1)
                last = act.wait_ge(off_parts, 4 * (2 * l + p + 1))
                act.sem_inc(acc_free, 1)

            def split_offsets(l):
                for b in range(B):
                    act.wait_ge(off_sum, B * l + b + 1)
                    if l:
                        act.wait_ge(tx_abs, 54 * l)
                        act.wait_ge(t_full[1], (T_LAYER * l + T_MAIN) // 2 - 1 - ITEMS // 2)
                    nc.scalar.activation(pos[0:OFF, b, :], off_b[:, b, :], ACT.Copy).then_inc(pos_high, 1)
                if l:
                    for b in range(B):
                        act.wait_ge(omax_ready, B + 1 + B)
                        nc.scalar.activation(off_a[:, b, :], off_a[:, b, :], ACT.Sigmoid).then_inc(sig_ready, 1)
                    for b in range(B):
                        act.wait_ge(sig_ready, b + 1)
                        act.wait_ge(cleared, 5)
                        nc.scalar.activation(msk[0:OFF, b, :], off_a[:, b, :], ACT.Copy).then_inc(msk_high, 1)

            def z_out(l):
                for i in range(B * CHUNKS):
                    b, j = divmod(i, CHUNKS)
                    n = T_LAYER * l + T_Z + i
                    act.wait_ge(t_full[n % 2], n // 2 + 1)
                    q = pixels(j)
                    v = tbuf(n)[0:q].rearrange("p (h c) -> p h c", h=2)[:, :, 0:HALF]
                    nc.scalar.activation(z[0:q, b, j, :].rearrange("p (h c) -> p h c", h=2), v, ACT.Copy)\
                        .then_inc(z_ready, 1)
                    act.wait_ge(z_ready, B * CHUNKS * l + i + 1)
                    act.sem_inc(t_free[n % 2], 1)

            def y_tents(l):
                for i in range(PAIRS * CHUNKS):
                    p, j = divmod(i, CHUNKS)
                    m = PAIRS * CHUNKS * l + i
                    n = T_LAYER * l + T_Y + i
                    nw = (wide(j)[1] - wide(j)[0]) * W
                    act.wait_ge(t_full[n % 2], n // 2 + 1)
                    v = tbuf(n)[0:YROWS].rearrange("p (b c) -> p b c", b=2)[:, :, 0:nw]
                    nc.scalar.activation(ya[:, m % 2, :, 0:nw], v, ACT.Abs).then_inc(act_c, 1)
                    act.wait_ge(act_c, m + 1)
                    act.sem_inc(t_free[n % 2], 1)
                    if m >= 2:
                        act.wait_ge(ytent_ready, m - 1)
                    nc.scalar.activation(yt[:, m % 2, :, 0:nw], ya[:, m % 2, :, 0:nw], ACT.Relu, scale=-1.0, bias=1.0)\
                        .then_inc(yt_ready, 1)
                    if l:
                        act.wait_ge(ym_ready, i + 1)
                        src = ym
                    else:
                        act.wait_ge(yt_ready, m + 1)
                        src = yt
                    nc.scalar.activation(yh[:, m % 2, :, 0:nw], src[:, m % 2, :, 0:nw], ACT.Copy).then_inc(yh_ready, 1)

            def x_tents(l, u):
                for kx in range(3):
                    for c in range(3):
                        n = XJ[(l, "tx", u, kx, c)]
                        g = 3 * PAIRS * l + u
                        if g >= TX_SLOTS:
                            act.wait_ge(s_ready, UNIT_ITEMS * (g - TX_SLOTS + 1))
                        act.wait_ge(xb_full[n % 2], n // 2 + 1)
                        nc.scalar.activation(tx[:, u % TX_SLOTS, kx, TXCHUNK * c:TXCHUNK * (c + 1)],
                                             xb[0:ROWS * W, n % 2, 0:TXCHUNK], ACT.Abs).then_inc(tx_abs, 1)
                        act.wait_ge(tx_abs, 54 * l + 9 * u + 3 * kx + c + 1)
                        act.sem_inc(xb_free[n % 2], 1)

            def acc_out(l, p):
                act.wait_ge(acc_full, 4 * l + 2 + p + 1)
                if l:
                    act.wait_ge(x_mid_ready, 2 * B)
                nc.scalar.activation(y[:, p, :].rearrange("o (h c) -> o h c", h=2), acc[:, :, 0:HALF], ACT.Identity,
                                     scale=w_neg[:, l:l + 1], bias=vec[:, 2 + l:3 + l])\
                    .then_inc(y_ready, 1)
                act.wait_ge(y_ready, PAIRS * l + p + 1)
                act.sem_inc(acc_free, 1)

            def general(l):
                na, nd, np_ = g_steps(l)
                with act.Fori(0, PAIRS) as p:
                    with act.Fori(0, TAPS) as k:
                        for bb in range(2):
                            it = 2 * (TAPS * p + k) + bb
                            b = 2 * p + bb
                            act.wait_ge(g_pe[l], np_ * it)
                            copies = [(g_pos[:, :], pos[0:KPOS, bass.ds(b, 1), :]),
                                      (g_ex[:, :], ex[:, bass.ds(k, 1), :]), (g_ef[:, :], ef[:, bass.ds(k, 1), :]),
                                      (g_z[:, 0:4 * C].rearrange("q (j o) -> q j o", j=4), None),
                                      (g_z[0:pixels(4), 4 * C:5 * C], None)]
                            if l:
                                copies += [(g_msk[:, :], msk[0:KMASK, bass.ds(b, 1), :]),
                                           (g_em[:, :], em[:, bass.ds(k, 1), :])]
                            zf = z[:, :, :, :].rearrange("q b j (k o) -> q b j k o", k=TAPS)
                            for i, (dst, src) in enumerate(copies):
                                if i == 3:
                                    src = zf[:, bass.ds(b, 1), 0:4, bass.ds(k, 1), :]
                                elif i == 4:
                                    src = zf[0:pixels(4), bass.ds(b, 1), 4, bass.ds(k, 1), :]
                                nc.scalar.activation(dst, src, ACT.Copy).then_inc(g_act[l], 1)
                            act.wait_ge(g_pe[l], np_ * it + 1)
                            nc.scalar.activation(halves(g_xt), halves(tbuf(0))[0:ROWS * W, :, 0:HALF], ACT.Abs)\
                                .then_inc(g_act[l], 1)
                            act.wait_ge(g_act[l], na * it + 6 + 2 * l)
                            nc.scalar.activation(g_xt, g_xt, ACT.Relu, scale=-1.0, bias=1.0).then_inc(g_act[l], 1)
                            for j in range(CHUNKS):
                                act.wait_ge(g_pe[l], np_ * it + 2 + 2 * j)
                                nc.scalar.activation(halves(g_yt), halves(tbuf(1))[0:ROWS * W, :, 0:HALF], ACT.Abs,
                                                     bias=full[0:ROWS * W, 514 + j:515 + j]).then_inc(g_act[l], 1)
                    act.wait_ge(g_sum[l], p + 1)
                    nc.scalar.activation(halves(y[:, bass.ds(p, 1), :].rearrange("o a c -> o (a c)")),
                                         acc[:, :, 0:HALF], ACT.Identity,
                                         scale=w_neg[:, l:l + 1], bias=vec[:, 2 + l:3 + l]).then_inc(g_out[l], 1)
                act.wait_ge(g_out[l], PAIRS)

            for l in range(LAYERS):
                weights(l)
                split_x(l)
                offsets(l, 0)
                offsets(l, 1)
                split_offsets(l)
                z_out(l)
                y_tents(l)
                for u in range(3 * PAIRS):
                    x_tents(l, u)
                    if u == 3:
                        acc_out(l, 0)
                acc_out(l, 1)
                with act.If(g_flag(act, l) != 0):
                    general(l)
            for p in range(PAIRS):
                act.wait_ge(fin_ready, 1)
                nc.scalar.activation(res[:, p, :], y[:, p, :], ACT.Relu, scale=fin[:, 6, p:p + 1], bias=fin[:, 7, p:p + 1])\
                    .then_inc(relu_ready, 1)

        @block.vector
        def _(dve):
            count = [0]

            def then(ins):
                count[0] += 1
                ins.then_inc(dve_c, 1)
                dve.wait_ge(dve_c, count[0])

            def scale_weights(l):
                for i in range(2):
                    m = slice(2 * l + i, 2 * l + i + 1)
                    dve.wait_ge(w_here[l][i], 16)
                    then(nc.vector.tensor_reduce(w_max[:, m], w_raw[l][i][:, :], axis=AX.X, op=ALU.max,
                                                 apply_absolute_value=True))
                    then(nc.vector.tensor_scalar(w_max[:, m], w_max[:, m], 1e-30, None, ALU.max))
                    then(nc.vector.reciprocal(w_inv[:, m], w_max[:, m]))
                    if l:
                        dve.wait_ge(wt_high, 2)
                    for d in range(2):
                        nc.vector.tensor_scalar(w_unit[i][:, :, d, :],
                                                w_raw[l][i][:, :].rearrange("o (t c) -> o t c", t=TAPS),
                                                w_inv[:, m], None, ALU.mult).then_inc(w_scaled, 1)
                then(nc.vector.tensor_scalar(w_neg[:, l:l + 1], w_max[:, 2 * l + 1:2 * l + 2], -1.0, None, ALU.mult))

            def split_weights(l):
                n = T_LAYER * l + T_WT
                dve.wait_ge(wt_high, 2 * l + 1)
                v = tbuf(n)[:, 0:TAPS * 64].rearrange("p (t o) -> p t o", t=TAPS)[:, :, 32:64]
                nc.vector.tensor_tensor(w_off16[:, :, 32:64], v, w_off16[:, :, 0:32], ALU.subtract).then_inc(wt_done, 1)
                dve.wait_ge(wt_done, 2 * l + 1)
                dve.sem_inc(t_free[n % 2], 1)
                n += 1
                dve.wait_ge(wt_high, 2 * l + 2)
                nc.vector.tensor_tensor(w_lo[:, :], tbuf(n)[:, 0:TAPS * C], w_hi[:, :], ALU.subtract).then_inc(wt_done, 1)
                dve.wait_ge(wt_done, 2 * l + 2)
                dve.sem_inc(t_free[n % 2], 1)

            def norm(l):
                for b in range(B):
                    if l == 0:
                        dve.wait_ge(x_here[b], 32)
                    for i in range(2):
                        nc.vector.bn_stats(bn[:, b, i, :], x_l[:, b, HALF * i:HALF * (i + 1)]).then_inc(dve_c, 1)
                count[0] += 2 * B
                dve.wait_ge(dve_c, count[0])
                for b in range(B):
                    nc.vector.bn_aggr(chan[:, :, b], bn[:, b, :, :]).then_inc(stats_ready, 1)
                n = XJ[(l, "norm")]
                dve.wait_ge(xb_full[n % 2], n // 2 + 1)
                then(nc.vector.tensor_copy(group[:, :, :], xb[:, n % 2, 0:3 * B].rearrange("p (a b) -> p a b", a=3)))
                dve.sem_inc(xb_free[n % 2], 1)
                then(nc.vector.tensor_tensor(gsq[:, :], group[:, 2, :], group[:, 2, :], ALU.mult))
                then(nc.vector.tensor_tensor(gsq[:, :], gsq[:, :], group[:, 1, :], ALU.add))
                nc.vector.tensor_scalar(gvar[:, :], gsq[:, :], GN_EPS, None, ALU.add).then_inc(gvar_ready, 1)
                dve.wait_ge(rstd_ready, l + 1)
                for b in range(B):
                    nc.vector.tensor_scalar(xn[:, b, :], x_l[:, b, :], group[:, 0, b:b + 1], rstd[:, b:b + 1],
                                            ALU.subtract, ALU.mult).then_inc(xn_ready, 1)
                for b in range(B):
                    dve.wait_ge(xn_ready, B * l + b + 1)
                    dve.wait_ge(xh_ready, B * l + b + 1)
                    nc.vector.scalar_tensor_tensor(out=xh[:, b, :], in0=xh[:, b, :], scalar=low_c, in1=xn[:, b, :],
                                                   op0=ALU.mult, op1=ALU.add).then_inc(x16_ready, 1)

            def sum_offsets(l):
                for b in range(B):
                    dve.wait_ge(off_parts, 2 * (B * l + b + 1))
                    then(nc.vector.tensor_tensor(off_a[:, b, :], off_a[:, b, :], off_b[:, b, :], ALU.add))
                    nc.vector.tensor_scalar(off_b[:, b, :], off_a[:, b, :], -BIG, BIG, ALU.max, ALU.min).then_inc(off_sum, 1)
                    nc.vector.tensor_reduce(omax[0:NOFF, b:b + 1], off_a[0:NOFF, b, :], axis=AX.X, op=ALU.max,
                                            apply_absolute_value=True).then_inc(omax_ready, 1)
                for b in range(B):
                    dve.wait_ge(pos_high, B * l + b + 1)
                    nc.vector.tensor_tensor(pos[LO:LO + OFF, b, :], off_b[:, b, :], pos[0:OFF, b, :], ALU.subtract)\
                        .then_inc(pos_ready, 1)
                if l:
                    for b in range(B):
                        dve.wait_ge(msk_high, b + 1)
                        nc.vector.tensor_tensor(msk[LO:LO + OFF, b, :], off_a[:, b, :], msk[0:OFF, b, :], ALU.subtract)\
                            .then_inc(msk_ready, 1)

            def find_flag(l):
                dve.wait_ge(omax_ready, (B + 1) * l + B)
                nc.vector.tensor_reduce(omax1[0:NOFF, :], omax[0:NOFF, :], axis=AX.X, op=ALU.max).then_inc(omax_ready, 1)
                n = XJ[(l, "flag")]
                dve.wait_ge(xb_full[n % 2], n // 2 + 1)
                then(nc.vector.tensor_reduce(oall[:, :], xb[0:1, n % 2, 0:NOFF], axis=AX.X, op=ALU.max))
                dve.sem_inc(xb_free[n % 2], 1)
                nc.vector.tensor_scalar(flag[:, l:l + 1], oall[:, :], float(REACH), None, ALU.is_gt).then_inc(flag_ready, 1)

            def y_tents(l):
                for i in range(PAIRS * CHUNKS):
                    p, j = divmod(i, CHUNKS)
                    m = PAIRS * CHUNKS * l + i
                    nw = (wide(j)[1] - wide(j)[0]) * W
                    src = yt
                    if l:
                        dve.wait_ge(yt_ready, m + 1)
                        for bb in range(2):
                            n = XJ[(l, "mask", p, j, bb)]
                            dve.wait_ge(xb_full[n % 2], n // 2 + 1)
                            nc.vector.tensor_tensor(ym[:, m % 2, bb, 0:nw], xb[0:YROWS, n % 2, 0:nw],
                                                    yt[:, m % 2, bb, 0:nw], ALU.mult).then_inc(xb_free[n % 2], 1)
                            dve.wait_ge(xb_free[n % 2], n // 2 + 1)
                        dve.sem_inc(ym_ready, 1)
                        src = ym
                    dve.wait_ge(yh_ready, m + 1)
                    nc.vector.scalar_tensor_tensor(
                        out=ytent[:, 2 * p:2 * p + 2, WIDE_AT[j]:WIDE_AT[j] + nw], in0=yh[:, m % 2, :, 0:nw],
                        scalar=low_y, in1=src[:, m % 2, :, 0:nw], op0=ALU.mult, op1=ALU.add).then_inc(ytent_ready, 1)

            def sampling(l):
                for g, (p, ky, j) in enumerate(STEPS):
                    u, q = 3 * p + ky, pixels(j)
                    r0, r1 = band(j, ky)
                    nb = (r1 - r0) * W
                    for bb in range(2):
                        i = 2 * g + bb
                        m = ITEMS * l + i
                        n = T_LAYER * l + T_MAIN + i
                        dve.wait_ge(tx_ready, 3 * (3 * PAIRS * l + u + 1))
                        if m >= S_SLOTS:
                            dve.wait_ge(s_used, m // 2 - S_SLOTS // 2 + 1)
                        dve.wait_ge(t_full[n % 2], n // 2 + 1)
                        nc.vector.scalar_tensor_tensor(
                            out=s[0:q, m % S_SLOTS, :, 0:nb],
                            in0=tx[0:q, u % TX_SLOTS, :, HW * bb + W * r0:HW * bb + W * r1], scalar=1.0,
                            in1=tbuf(n)[0:q, 0:3 * SLOT].rearrange("p (k c) -> p k c", k=3)[:, :, 0:nb],
                            op0=ALU.subtract, op1=ALU.mult).then_inc(s_ready, 1)
                        dve.wait_ge(s_ready, m + 1)
                        dve.sem_inc(t_free[n % 2], 1)

            def general(l):
                na, nd, np_ = g_steps(l)
                with dve.Fori(0, PAIRS) as p:
                    with dve.Fori(0, TAPS) as k:
                        for bb in range(2):
                            it = 2 * (TAPS * p + k) + bb
                            for j in range(CHUNKS):
                                done = nd * it + (2 + l) * j
                                dve.wait_ge(g_act[l], na * it + 8 + 2 * l + j)
                                nc.vector.tensor_scalar(g_yt, g_yt, 1.0, 1.0, ALU.min, ALU.subtract)\
                                    .then_inc(g_dve[l], 1)
                                dve.wait_ge(g_dve[l], done + 1)
                                nc.vector.tensor_tensor(g_s, g_yt, g_xt, ALU.mult).then_inc(g_dve[l], 1)
                                if l:
                                    dve.wait_ge(g_dve[l], done + 2)
                                    nc.vector.tensor_tensor(halves(g_s), xb[0:ROWS * W, :, 0:HALF], halves(g_s),
                                                            ALU.mult).then_inc(g_dve[l], 1)
                dve.wait_ge(g_out[l], PAIRS)

            dve.wait_ge(full_here, 16)
            dve.wait_ge(vec_here, 16)
            scale_weights(0)
            norm(0)
            split_weights(0)
            scale_weights(1)
            sum_offsets(0)
            y_tents(0)
            find_flag(0)
            sampling(0)
            dve.wait_ge(y_ready, PAIRS)
            with dve.If(g_flag(dve, 0) != 0):
                general(0)
            for p in range(PAIRS):
                dve.wait_ge(y_ready, p + 1)
                for bb in range(2):
                    r = slice(64 * bb, 64 * bb + 64)
                    for d in (1 - bb, bb):
                        nc.vector.tensor_tensor(x_l[64 * d:64 * d + 64, 2 * p + bb, :], y[r, p, :],
                                                x_l[r, 2 * p + bb, :], ALU.add).then_inc(x_mid_ready, 1)
            dve.wait_ge(x_mid_ready, 2 * B)
            norm(1)
            split_weights(1)
            sum_offsets(1)
            y_tents(1)
            find_flag(1)
            sampling(1)
            dve.wait_ge(y_ready, 2 * PAIRS)
            with dve.If(g_flag(dve, 1) != 0):
                general(1)
            for p in range(PAIRS):
                dve.wait_ge(y_ready, PAIRS + p + 1)
                for i in range(2):
                    nc.vector.bn_stats(bn[:, p, i, :], y[:, p, HALF * i:HALF * (i + 1)]).then_inc(dve_c, 1)
            count[0] += 2 * PAIRS
            dve.wait_ge(dve_c, count[0])
            for p in range(PAIRS):
                nc.vector.bn_aggr(fin[:, 0:2, p], bn[:, p, :, :]).then_inc(stats_ready, 1)
            n = XJ["final mean"]
            dve.wait_ge(xb_full[n % 2], n // 2 + 1)
            then(nc.vector.tensor_copy(fin[:, 2:4, :], xb[:, n % 2, 0:2 * PAIRS].rearrange("p (a b) -> p a b", a=2)))
            then(nc.vector.tensor_tensor(fin[:, 4, :], fin[:, 0, :], fin[:, 2, :], ALU.subtract))
            nc.vector.tensor_tensor(fin[:, 5, :], fin[:, 4, :], fin[:, 4, :], ALU.mult).then_inc(stats_ready, 1)
            n = XJ["final var"]
            dve.wait_ge(xb_full[n % 2], n // 2 + 1)
            then(nc.vector.tensor_tensor(fin[:, 3, :], xb[:, n % 2, 0:PAIRS], fin[:, 3, :], ALU.add))
            nc.vector.tensor_scalar(fin[:, 4, :], fin[:, 3, :], GN_EPS, None, ALU.add).then_inc(fin_in, 1)
            dve.wait_ge(rstd_ready, LAYERS + 1)
            then(nc.vector.tensor_scalar(fin[:, 6, :], fin[:, 5, :], vec[:, 4:5], None, ALU.mult))
            then(nc.vector.tensor_tensor(fin[:, 4, :], fin[:, 2, :], fin[:, 6, :], ALU.mult))
            nc.vector.tensor_scalar(fin[:, 7, :], fin[:, 4, :], -1.0, vec[:, 5:6], ALU.mult, ALU.add).then_inc(fin_ready, 1)
            for p in range(PAIRS):
                dve.wait_ge(relu_ready, p + 1)
                for bb in range(2):
                    r = slice(64 * bb, 64 * bb + 64)
                    nc.vector.tensor_tensor(res[r, p, :], res[r, p, :], x_l[r, 2 * p + bb, :], ALU.add).then_inc(res_ready, 1)

        @block.tensor
        def _(pe):
            mm = nc.tensor.matmul

            def t_take(n):
                if n >= 2:
                    pe.wait_ge(t_free[n % 2], n // 2)

            def x_take(n):
                if n >= 2:
                    pe.wait_ge(xb_free[n % 2], n // 2)

            def weights(l):
                for i in range(2):
                    n = T_LAYER * l + T_WT + i
                    pe.wait_ge(w_scaled, 4 * l + 2 * i + 2)
                    t_take(n)
                    for t in range(TAPS):
                        last = nc.tensor.transpose(tbuf(n)[:, 64 * t:64 * t + 64], w_unit[i][0:64, t, :, :],
                                                   ident[0:64, 0:64])
                    last.then_inc(t_full[n % 2], 1)

            def norm(l):
                n = XJ[(l, "norm")]
                pe.wait_ge(stats_ready, B * (l + 1))
                x_take(n)
                v = chan[:, :, :]
                mm(xb[:, n % 2, 0:2 * B], pair_m, v, start=True, stop=True)
                mm(xb[:, n % 2, 2 * B:3 * B], diff_m, chan[:, 0, :], start=True, stop=True).then_inc(xb_full[n % 2], 1)

            def conv(l, p):
                pe.wait_ge(wt_done, 2 * l + 1)
                pe.wait_ge(xpad_ready, B * l + 2 * p + 2)
                if 4 * l + p:
                    pe.wait_ge(acc_free, 4 * l + p)
                for t in range(TAPS):
                    ty, tx_ = divmod(t, 3)
                    for hf in range(2):
                        for bb in range(2):
                            last = mm(acc[64 * bb:64 * bb + 64, hf, 0:HALF], w_off16[:, t, :],
                                      xpad_v[:, 2 * p + bb, 12 * hf + ty:12 * hf + ty + 12, tx_:tx_ + W],
                                      start=t == 0, stop=t == TAPS - 1)
                last.then_inc(acc_full, 1)

            def z_products(l, lo, hi):
                pe.wait_ge(wt_done, 2 * l + 2)
                for i in range(lo, hi):
                    b, j = divmod(i, CHUNKS)
                    n = T_LAYER * l + T_Z + i
                    q = pixels(j)
                    pe.wait_ge(x16_ready, B * l + b + 1)
                    t_take(n)
                    pix = xh[:, b, ROWS * W * j:ROWS * W * j + q]
                    for hf in range(2):
                        for part, wp in enumerate((w_hi, w_lo)):
                            last = mm(tbuf(n)[0:q, BANK * hf:BANK * hf + HALF], pix, wp[:, HALF * hf:HALF * (hf + 1)],
                                      start=part == 0, stop=part == 1)
                    last.then_inc(t_full[n % 2], 1)

            def y_distances(l):
                pe.wait_ge(half_here, 16)
                pe.wait_ge(pos_here, 16)
                pe.wait_ge(pos_ready, B * (l + 1))
                if l:
                    pe.wait_ge(msk_ready, B)
                for i in range(PAIRS * CHUNKS):
                    p, j = divmod(i, CHUNKS)
                    n = T_LAYER * l + T_Y + i
                    r0, r1 = wide(j)
                    t_take(n)
                    for bb in range(2):
                        last = mm(tbuf(n)[0:YROWS, BANK * bb:BANK * bb + (r1 - r0) * W], ey[0:KPOS, j, :],
                                  pos[0:KPOS, 2 * p + bb, W * r0:W * r1], start=True, stop=True)
                    last.then_inc(t_full[n % 2], 1)
                    if l:
                        for bb in range(2):
                            m = XJ[(l, "mask", p, j, bb)]
                            x_take(m)
                            mm(xb[0:YROWS, m % 2, 0:(r1 - r0) * W], my[0:KMASK, 0, :],
                               msk[0:KMASK, 2 * p + bb, W * r0:W * r1], start=True, stop=True).then_inc(xb_full[m % 2], 1)

            def x_distance(l, u, kx, c):
                n = XJ[(l, "tx", u, kx, c)]
                p, ky = divmod(u, 3)
                x_take(n)
                v = pos[0:KPOS, :, :].rearrange("r b c -> r (b c)")
                at = 2 * p * HW + TXCHUNK * c
                mm(xb[0:ROWS * W, n % 2, 0:TXCHUNK], ex[0:KPOS, 3 * ky + kx, :], v[:, at:at + TXCHUNK],
                   start=True, stop=True).then_inc(xb_full[n % 2], 1)

            def spread_rows(l, g, bb):
                p, ky, j = STEPS[g]
                i = 2 * g + bb
                n = T_LAYER * l + T_MAIN + i
                r0, r1 = band(j, ky)
                at = WIDE_AT[j] + W * (r0 - wide(j)[0])
                t_take(n)
                for kx in range(3):
                    last = mm(tbuf(n)[0:pixels(j), SLOT * kx:SLOT * kx + W * (r1 - r0)],
                              sel[0:YROWS, 3 * ky + kx, 0:pixels(j)],
                              ytent[:, 2 * p + bb, at:at + W * (r1 - r0)], start=True, stop=True)
                last.then_inc(t_full[n % 2], 1)

            def products(l, g):
                p, ky, j = STEPS[g]
                q = pixels(j)
                r0, r1 = band(j, ky)
                first, final = g % (3 * CHUNKS) == 0, g % (3 * CHUNKS) == 3 * CHUNKS - 1
                if first:
                    pe.wait_ge(acc_free, 4 * l + 2 + p)
                    for hf in range(2):
                        mm(acc[:, hf, 0:HALF], zeros[0:1, 0:128], zeros[0:1, 0:HALF], start=True, stop=False,
                           skip_group_check=True)
                pe.wait_ge(s_ready, ITEMS * l + 2 * g + 2)
                pieces = [(max(r0, 12 * hf), min(r1, 12 * hf + 12), hf) for hf in range(2)]
                for kx in range(3):
                    for a, b, hf in pieces:
                        if a >= b:
                            continue
                        for bb in range(2):
                            m = ITEMS * l + 2 * g + bb
                            k = 3 * ky + kx
                            last = mm(acc[64 * bb:64 * bb + 64, hf, W * (a - 12 * hf):W * (b - 12 * hf)],
                                      z[0:q, 2 * p + bb, j, 64 * k:64 * k + 64],
                                      s[0:q, m % S_SLOTS, kx, W * (a - r0):W * (b - r0)],
                                      start=False, stop=final and kx == 2, skip_group_check=True)
                last.then_inc(s_used, 1)
                if final:
                    nc_last = pe.wait_ge(s_used, len(STEPS) * l + g + 1)
                    pe.sem_inc(acc_full, 1)

            def general(l):
                na, nd, np_ = g_steps(l)
                with pe.Fori(0, PAIRS) as p:
                    pe.wait_ge(g_out[l], p)
                    for hf in range(2):
                        last = mm(acc[:, hf, 0:HALF], zeros[0:1, 0:128], zeros[0:1, 0:HALF], start=True, stop=False,
                                  skip_group_check=True)
                    with pe.Fori(0, TAPS) as k:
                        for bb in range(2):
                            it = 2 * (TAPS * p + k) + bb
                            pe.wait_ge(g_act[l], na * it + 5 + 2 * l)
                            for hf in range(2):
                                last = mm(tbuf(0)[0:ROWS * W, BANK * hf:BANK * hf + HALF], g_ex[0:KPOS, :],
                                          g_pos[:, HALF * hf:HALF * (hf + 1)], start=True, stop=True)
                            last.then_inc(g_pe[l], 1)
                            for j in range(CHUNKS):
                                q = pixels(j)
                                pe.wait_ge(g_dve[l], nd * it + (2 + l) * j)
                                for hf in range(2):
                                    c = slice(HALF * hf, HALF * (hf + 1))
                                    last = mm(tbuf(1)[0:ROWS * W, BANK * hf:BANK * hf + HALF], g_ef[0:KPOS, :],
                                              g_pos[:, c], start=True, stop=True)
                                    if l:
                                        last = mm(xb[0:ROWS * W, hf, 0:HALF], g_em[0:KMASK, :], g_msk[:, c],
                                                  start=True, stop=True)
                                last.then_inc(g_pe[l], 1)
                                pe.wait_ge(g_dve[l], nd * it + (2 + l) * (j + 1))
                                for hf in range(2):
                                    last = mm(acc[64 * bb:64 * bb + 64, hf, 0:HALF], g_z[0:q, C * j:C * (j + 1)],
                                              g_s[0:q, HALF * hf:HALF * (hf + 1)], start=False, stop=False,
                                              skip_group_check=True)
                                last.then_inc(g_pe[l], 1)
                    pe.wait_ge(g_pe[l], np_ * 2 * TAPS * (p + 1))
                    pe.sem_inc(g_sum[l], 1)
                pe.wait_ge(g_out[l], PAIRS)

            pe.wait_ge(full_here, 16)
            for l in range(LAYERS):
                weights(l)
                norm(l)
                conv(l, 0)
                z_products(l, 0, 2)
                conv(l, 1)
                z_products(l, 2, B * CHUNKS)
                y_distances(l)
                n = XJ[(l, "flag")]
                pe.wait_ge(omax_ready, (B + 1) * (l + 1))
                x_take(n)
                nc.tensor.transpose(xb[0:1, n % 2, 0:NOFF], omax1[0:NOFF, :], ident[0:NOFF, 0:NOFF])\
                    .then_inc(xb_full[n % 2], 1)
                pe.wait_ge(z_ready, B * CHUNKS * (l + 1))
                pe.wait_ge(ytent_ready, PAIRS * CHUNKS * (l + 1))
                jobs = {u: [(kx, c) for kx in range(3) for c in range(3)] for u in range(3 * PAIRS)}
                for kx, c in jobs[0]:
                    x_distance(l, 0, kx, c)
                spread_rows(l, 0, 0)
                spread_rows(l, 0, 1)
                for g in range(len(STEPS)):
                    u, at = divmod(g, CHUNKS)
                    if g + 1 < len(STEPS):
                        spread_rows(l, g + 1, 0)
                        spread_rows(l, g + 1, 1)
                    products(l, g)
                    if u + 1 < 3 * PAIRS:
                        for kx, c in jobs[u + 1][2 * at:2 * at + 2]:
                            x_distance(l, u + 1, kx, c)
                pe.wait_ge(y_ready, PAIRS * (l + 1))
                with pe.If(g_flag(pe, l) != 0):
                    general(l)
            pe.wait_ge(stats_ready, B * LAYERS + PAIRS)
            n = XJ["final mean"]
            x_take(n)
            mm(xb[:, n % 2, 0:2 * PAIRS], block_m, fin[:, 0:2, :], start=True, stop=True).then_inc(xb_full[n % 2], 1)
            pe.wait_ge(stats_ready, B * LAYERS + PAIRS + 1)
            n = XJ["final var"]
            x_take(n)
            mm(xb[:, n % 2, 0:PAIRS], block_m, fin[:, 5, :], start=True, stop=True).then_inc(xb_full[n % 2], 1)


def kernel(x, L0_conv_w_off, L0_conv_b_off, L0_conv_w_def, L0_conv_b_def,
           L1_conv_w_off, L1_conv_b_off, L1_conv_w, L1_conv_b, L1_conv_gamma, L1_conv_beta):
    import concourse.bacc as bacc
    from concourse.bass_utils import run_bass_kernel_spmd

    def off_rows(a):
        a = np.asarray(a)
        return np.tile(np.pad(a, [(0, 32 - a.shape[0])] + [(0, 0)] * (a.ndim - 1)), [4] + [1] * (a.ndim - 1))

    def taps(w):
        w = np.asarray(w)
        return w.transpose(0, 2, 3, 1).reshape(w.shape[0], TAPS * C)

    def twice(a):
        a = np.asarray(a)
        return np.concatenate([a, a], 0)

    half, full, pos = constants()
    vecs = np.stack([off_rows(L0_conv_b_off), off_rows(L1_conv_b_off), twice(L0_conv_b_def), twice(L1_conv_b),
                     twice(L1_conv_gamma), twice(L1_conv_beta)], 1)
    arrays = {
        "x": np.ascontiguousarray(np.asarray(x).reshape(B, C, HW)),
        "w_off": np.ascontiguousarray(np.stack([off_rows(taps(L0_conv_w_off)), off_rows(taps(L1_conv_w_off))])),
        "w_def": np.ascontiguousarray(np.stack([twice(taps(L0_conv_w_def)), twice(taps(L1_conv_w))])),
        "vecs": np.ascontiguousarray(vecs), "c_half": half, "c_full": full, "c_pos": np.ascontiguousarray(pos),
    }
    nc = bacc.Bacc("TRN2", target_bir_lowering=False, num_devices=1)
    args = {n: nc.dram_tensor(n, a.shape, mybir.dt.from_np(a.dtype), kind="ExternalInput").ap() for n, a in arrays.items()}
    out = nc.dram_tensor("out", (B, C, HW), F32, kind="ExternalOutput").ap()
    build(nc, out=out, **args)
    r = run_bass_kernel_spmd(nc, [arrays], core_ids=[0])
    return r.results[0]["out"].reshape(B, C, H, W)
```

```python
from contextlib import ExitStack

import numpy as np

import concourse.bass as bass
from concourse import mybir

F32, F16, I32 = mybir.dt.float32, mybir.dt.float16, mybir.dt.int32
ALU = mybir.AluOpType
ACT = mybir.ActivationFunctionType
AX = mybir.AxisListType

B, C, H, W = 4, 64, 24, 24
HW = H * W
TAPS = 9
LAYERS = 2
PAIRS = B // 2
HALF = HW // 2
PADW = W + 2
BANK = 512

ROWS = 5
CHUNKS = -(-H // ROWS)
REACH = 2
BIG = 32.0
OFF = 27
NOFF = 2 * TAPS
LO = 32
KPOS = 67
KMASK = LO + OFF
YROWS = 2 * TAPS * ROWS
GN_EPS = 1e-5


def pixels(j):
    return W * (min(H, ROWS * (j + 1)) - ROWS * j)


def band(j, ky):
    a, b = ROWS * j, min(H, ROWS * (j + 1)) - 1
    return max(0, a - REACH - (ky - 1)), min(H, b + REACH - (ky - 1) + 1)


def wide(j):
    return min(band(j, ky)[0] for ky in range(3)), max(band(j, ky)[1] for ky in range(3))


WIDE_AT = [sum(wide(i)[1] - wide(i)[0] for i in range(j)) * W for j in range(CHUNKS + 1)]
WIDEST = max(wide(j)[1] - wide(j)[0] for j in range(CHUNKS)) * W
BANDEST = max(band(j, ky)[1] - band(j, ky)[0] for j in range(CHUNKS) for ky in range(3)) * W
SLOT = 256
assert BANDEST <= SLOT and WIDEST <= BANK

STAGES = LAYERS * PAIRS
STEPS = [(ky, j) for ky in range(3) for j in range(CHUNKS)]
NSTEPS = len(STEPS)
ITEMS = 2 * NSTEPS
TX_SLOTS, S_SLOTS, T_BUFS = 3, 4, 3
POOL_KY = (1,)


def tx6(m, ky):
    return [("tx", m, (ky, kx, bb)) for kx in range(3) for bb in range(2)]


def before():
    return ([("weights", 0, 0), ("stats", 0, 0), ("norm", 0, 0), ("split", 0, 0), ("conv", 0, 0)]
            + [("z", 0, 0), ("offsets", 0, 0), ("z", 0, 1), ("position", 0, 0), ("z", 0, 2), ("z", 0, 3)]
            + [("y", 0, 0), ("y", 0, 1), ("y end", 0, 0)] + tx6(0, 0)[:2] + [("y", 0, 2), ("y end", 0, 1)]
            + tx6(0, 0)[2:] + [("y end", 0, 2)])


def during(m):
    return [sorted(parts, key=lambda part: part[0] != "tx") for parts in placed(m)]


def placed(m):
    at = [[] for _ in STEPS]
    for i, job in enumerate(tx6(m, 2)):
        at[i // 2 + (3 if m == 0 else 0)].append(job)
    if m == 0:
        for i, job in enumerate(tx6(0, 1)):
            at[i // 2].append(job)
        for i in range(3):
            at[i] += [("z", 0, 2 * i + 4), ("z", 0, 2 * i + 5)]
        at[0] += [("y", 0, 3)]
        at[1] += [("y end", 0, 3), ("y", 0, 4)]
        at[2] += [("y end", 0, 4), ("flag", 0, 0)]
        at[14] += [("weights", 1, 0)]
    if m == STAGES - 1:
        at[2] += [("final mean", m - 1, 0), ("final spread", m - 1, 0)]
        at[3] += [("final variance", m - 1, 0), ("final scale", m - 1, 0)]
        at[5] += [("final out", m - 1, 0)]
        return at
    n = m + 1
    at[0] += [("stats", n, 0)]
    at[1] += [("norm", n, 0)]
    at[2] += [("split", n, 0)]
    at[3] += [("conv", n, 0), ("offsets", n, 0)]
    at[4] += [("z", n, 0)]
    at[5] += [("position", n, 0), ("z", n, 1)]
    at[6] += [("z", n, 2), ("z", n, 3)]
    for j in range(CHUNKS):
        at[7 + j] += [("y", n, j), ("z", n, 4 + j)]
        at[8 + j] += [("y end", n, j)]
    at[12] += [("z", n, 9)]
    at[12] += [("flag", n, 0)]
    for i, job in enumerate(tx6(n, 0) + tx6(n, 1)):
        at[8 + i // 2].append(job)
    return at


def t_jobs():
    jobs = {}

    def add(part, m, a):
        if part == "weights":
            names = [("weights", m, i) for i in range(2)]
        elif part == "y":
            names = [("y", m, a)] + [("mask", m, a)] * (m >= PAIRS)
        elif part in ("norm", "conv", "z", "tx", "flag", "final mean", "final variance"):
            names = [(part, m, a)]
        else:
            names = []
        for n in names:
            jobs[n] = len(jobs)

    for part in before():
        add(*part)
    for m in range(STAGES):
        jobs["item", m, 0] = len(jobs)
        jobs["item", m, 1] = len(jobs)
        for g, parts in enumerate(during(m)):
            for part in parts:
                if part[0] == "tx":
                    add(*part)
            if g + 1 < NSTEPS:
                jobs["item", m, 2 * g + 2] = len(jobs)
                jobs["item", m, 2 * g + 3] = len(jobs)
            for part in parts:
                if part[0] != "tx":
                    add(*part)
    for part in ("final mean", "final variance"):
        add(part, STAGES - 1, 0)
    return jobs


JOB = t_jobs()


def constants():
    q_row, q_col = np.arange(ROWS * W) // W, np.arange(ROWS * W) % W
    ex = np.zeros((128, TAPS, ROWS * W), np.float16)
    ef = np.zeros((128, TAPS, ROWS * W), np.float16)
    em = np.zeros((128, TAPS, ROWS * W), np.float16)
    for k in range(TAPS):
        ex[[2 * k + 1, LO + 2 * k + 1, 65], k] = 1
        ex[66, k] = k % 3 - 1 - q_col
        ef[[2 * k, LO + 2 * k, 64], k] = 1
        ef[66, k] = k // 3 - 1 - q_row
        em[[NOFF + k, LO + NOFF + k], k] = 1
    ey = np.zeros((128, CHUNKS, 2, TAPS, ROWS), np.float16)
    my = np.zeros((128, 2, TAPS, ROWS), np.float16)
    sel = np.zeros((128, TAPS, ROWS * W), np.float16)
    for k in range(TAPS):
        ey[[2 * k, LO + 2 * k, 64], :, :, k] = 1
        for j in range(CHUNKS):
            ey[66, j, :, k] = k // 3 - 1 - (ROWS * j + np.arange(ROWS))
        my[[NOFF + k, LO + NOFF + k], :, k] = 1
        for part in range(2):
            for i in range(ROWS):
                sel[(part * TAPS + k) * ROWS + i, k, q_row == i] = 1
    half = np.concatenate([a.reshape(128, -1) for a in (ex, ey, my, sel, ef, em)], 1)
    at = np.arange(128)
    same = at[:, None] // 2 == at[None, :] // 2
    ident = np.eye(128, dtype=np.float32)
    pair = np.where(same, 0.5, 0).astype(np.float32)
    diff = np.where(same, -0.5, 0).astype(np.float32) + ident
    block = np.where(at[:, None] // C == at[None, :] // C, 1 / C, 0).astype(np.float32)
    low = np.stack([at >= C, at >= TAPS * ROWS], 1) * np.float32(-1)
    rows = np.tile(-ROWS * np.arange(CHUNKS, dtype=np.float32), (128, 1))
    full = np.concatenate([ident, pair, diff, block, low, rows], 1)
    p = np.arange(HW)
    pos = np.stack([p // W, p % W, np.ones(HW)]).astype(np.float16)
    return half, full, np.repeat(pos[:, None], B, 1)


NHALF = TAPS * ROWS * W
HALF_AT = np.cumsum([0, NHALF, CHUNKS * YROWS, YROWS, NHALF, NHALF, NHALF])


def build(nc, x, w_off, w_def, vecs, c_half, c_full, c_pos, out):
    ctx = ExitStack()
    with ctx:
        def sb(name, shape, dt=F32):
            return ctx.enter_context(nc.sbuf_tensor(name, shape, dt))

        def sem(name):
            return ctx.enter_context(nc.semaphore(name))

        x_l = sb("x_l", [128, B, HW])
        xn = sb("xn", [128, 2, HW])
        xh = sb("xh", [128, B, HW], F16)
        xpad = sb("xpad", [128, B, PADW * PADW], F16)
        xpad_v = xpad[:, :, :].rearrange("p b (h w) -> p b h w", h=PADW)
        w_raw = [[sb(f"w_raw{l}{i}", [128, TAPS * C]) for i in range(2)] for l in range(LAYERS)]
        w_unit = [sb(f"w_unit{i}", [128, TAPS, 2, C]) for i in range(2)]
        w_max = sb("w_max", [128, 2 * LAYERS])
        w_inv = sb("w_inv", [128, 2 * LAYERS])
        w_neg = sb("w_neg", [128, LAYERS])
        w_off16 = [sb(f"w_off16_{l}", [128, TAPS, 64], F16) for l in range(LAYERS)]
        w_hi = [sb(f"w_hi{l}", [128, TAPS * C], F16) for l in range(LAYERS)]
        w_lo = [sb(f"w_lo{l}", [128, TAPS * C], F16) for l in range(LAYERS)]
        vec = sb("vec", [128, 6])
        half = sb("half", [128, int(HALF_AT[-1])], F16)
        full = sb("full", [128, 4 * 128 + 2 + CHUNKS])
        bn = sb("bn", [128, STAGES, 2, 2, 6])
        chan = sb("chan", [128, STAGES, 2, 2])
        group = sb("group", [128, STAGES, 3, 2])
        gsq = sb("gsq", [128, STAGES, 2])
        gvar = sb("gvar", [128, STAGES, 2])
        rstd = sb("rstd", [128, STAGES, 2])
        minus_half = sb("minus_half", [128, 2])
        off_a = sb("off_a", [OFF, 2, HW])
        off_b = sb("off_b", [OFF, 2, HW])
        pos = sb("pos", [128, B, HW], F16)
        msk = sb("msk", [KMASK, B, HW], F16)
        omax = sb("omax", [OFF, STAGES, 2])
        omax1 = sb("omax1", [OFF, STAGES])
        oall = sb("oall", [1, STAGES])
        flag = sb("flag", [1, STAGES], I32)
        ya = sb("ya", [YROWS, 2, 2, WIDEST])
        yt = sb("yt", [YROWS, 2, 2, WIDEST])
        ym = sb("ym", [YROWS, 2, 2, WIDEST])
        yh = sb("yh", [YROWS, 2, 2, WIDEST], F16)
        ytent = sb("ytent", [YROWS, B, WIDE_AT[-1]], F16)
        z = sb("z", [ROWS * W, B, CHUNKS, TAPS * C])
        tx = sb("tx", [ROWS * W, TX_SLOTS, 3, 2 * HW])
        s = sb("s", [ROWS * W, S_SLOTS, 3, BANDEST])
        zeros = sb("zeros", [1, HALF], F16)
        y = sb("y", [128, PAIRS, HW])
        fin = sb("fin", [128, PAIRS, 8])
        res = sb("res", [128, PAIRS, HW])
        spare = tx[:, (3 * STAGES - 1) % TX_SLOTS]
        g_xt, g_yt, g_s, g_z = spare[:, 0, 0:HW], spare[:, 0, HW:2 * HW], spare[:, 1, 0:HW], spare[:, 2, 0:CHUNKS * C]
        g_pos, g_msk = (spare[0:n, 1, HW + i * HW // 2:HW + (i + 1) * HW // 2].bitcast(F16)
                        for i, n in enumerate((KPOS, KMASK)))
        g_ex, g_ef, g_em = (spare[0:n, 2, HW + 60 * i:HW + 60 * (i + 1)].bitcast(F16)
                            for i, n in enumerate((KPOS, KPOS, KMASK)))

        def h(i, shape):
            v = half[:, int(HALF_AT[i]):int(HALF_AT[i + 1])]
            return v.rearrange("p (a b) -> p a b", a=shape)
        ex, ey, my, sel, ef, em = h(0, TAPS), h(1, CHUNKS), h(2, 1), h(3, TAPS), h(4, TAPS), h(5, TAPS)
        ident, pair_m, diff_m, block_m = (full[:, 128 * i:128 * (i + 1)] for i in range(4))
        low_c, low_y = full[:, 512:513], full[0:YROWS, 513:514]

        tb = ctx.enter_context(nc.psum_tensor("tb", [128, T_BUFS, 2 * BANK], F32))
        acc = ctx.enter_context(nc.psum_tensor("acc", [128, 2, BANK], F32))

        x_here = [sem(f"x_here{b}") for b in range(B)]
        w_here = [[sem(f"w_here{l}{i}") for i in range(2)] for l in range(LAYERS)]
        vec_here, half_here, full_here = sem("vec_here"), sem("half_here"), sem("full_here")
        pos_here = sem("pos_here")
        cleared = sem("cleared")
        t_full = [sem(f"t_full{i}") for i in range(T_BUFS)]
        t_free = [sem(f"t_free{i}") for i in range(T_BUFS)]
        acc_full, acc_free = sem("acc_full"), sem("acc_free")
        dve_c = sem("dve_c")
        w_scaled = sem("w_scaled")
        wt_high, wt_done = sem("wt_high"), sem("wt_done")
        x_mid = sem("x_mid")
        stats_ready, gvar_ready, rstd_ready = sem("stats_ready"), sem("gvar_ready"), sem("rstd_ready")
        xn_ready, xh_ready, x16_ready = sem("xn_ready"), sem("xh_ready"), sem("x16_ready")
        xpad0, xpad1 = sem("xpad0"), sem("xpad1")
        off_parts = sem("off_parts")
        off_sum, omax_ready, flag_ready = sem("off_sum"), sem("omax_ready"), sem("flag_ready")
        pos_high, pos_ready = sem("pos_high"), sem("pos_ready")
        sig_ready, msk_high, msk_ready = sem("sig_ready"), sem("msk_high"), sem("msk_ready")
        ya_ready, yt_ready, ym_ready, yh_ready = sem("ya_ready"), sem("yt_ready"), sem("ym_ready"), sem("yh_ready")
        ytent_ready = sem("ytent_ready")
        z_ready = sem("z_ready")
        tx_abs, tx_act, tx_pool = sem("tx_abs"), sem("tx_act"), sem("tx_pool")
        s_ready, s_used = sem("s_ready"), sem("s_used")
        y_ready = sem("y_ready")
        fin_stats, fin_var, fin_rstd, fin_ready = sem("fin_stats"), sem("fin_var"), sem("fin_rstd"), sem("fin_ready")
        relu_ready, res_ready, stored = sem("relu_ready"), sem("res_ready"), sem("stored")
        g_act, g_dve, g_pe, g_sum, g_out = ([sem(f"{n}{m}") for m in range(STAGES)]
                                            for n in ("g_act", "g_dve", "g_pe", "g_sum", "g_out"))

        block = ctx.enter_context(nc.Block())

        def tbuf(name):
            return tb[:, JOB[name] % T_BUFS, :]

        def wait_full(eng, name):
            n = JOB[name]
            eng.wait_ge(t_full[n % T_BUFS], n // T_BUFS + 1)

        def free_of(name):
            return t_free[JOB[name] % T_BUFS]

        def halves(v):
            return v.rearrange("p (h c) -> p h c", h=2)

        def banks(v):
            return halves(v)[:, :, 0:HALF]

        def where(m):
            return m // PAIRS, m % PAIRS

        def tents_wait(eng, m, ky):
            units = [k in POOL_KY for _ in range(m) for k in range(3)] + [k in POOL_KY for k in range(ky + 1)]
            if ky in POOL_KY:
                eng.wait_ge(tx_pool, 6 * sum(units))
            else:
                eng.wait_ge(tx_act, 6 * (len(units) - sum(units)))

        def g_steps(l):
            return 7 + 2 * l + CHUNKS, CHUNKS * (2 + l), 1 + 2 * CHUNKS

        def far(eng, m):
            eng.wait_ge(flag_ready, m + 1)
            return eng.value_load(flag[0:1, m:m + 1], min_val=0, max_val=1) != 0

        @block.sync
        def _(sp):
            for b in range(B):
                for d in range(2):
                    sp.dma_start(x_l[64 * d:64 * d + 64, b, :], x[b]).then_inc(x_here[b], 16)
                if b == 1:
                    sp.dma_start(full[:, :], c_full).then_inc(full_here, 16)
                    sp.wait_ge(cleared, 2)
                    sp.dma_start(pos[64:KPOS, :, :], c_pos).then_inc(pos_here, 16)
            sp.dma_start(w_raw[1][0][:, :], w_off[1]).then_inc(w_here[1][0], 16)
            sp.dma_start(w_raw[1][1][:, :], w_def[1]).then_inc(w_here[1][1], 16)
            for p in range(PAIRS):
                sp.wait_ge(res_ready, 2 * p + 2)
                for bb in range(2):
                    sp.dma_start(out[2 * p + bb], res[64 * bb:64 * bb + 64, p, :]).then_inc(stored, 16)
            sp.wait_ge(stored, 16 * B)

        @block.gpsimd
        def _(pool):
            nc.gpsimd.memset(minus_half[:, :], -0.5).then_inc(cleared, 1)
            nc.gpsimd.memset(pos[:, :, :].bitcast(F32), 0.0).then_inc(cleared, 1)
            nc.gpsimd.memset(xpad[:, :, :].bitcast(F32), 0.0).then_inc(cleared, 1)
            nc.gpsimd.memset(zeros[:, :], 0.0).then_inc(cleared, 1)
            nc.gpsimd.memset(msk[:, :, :].bitcast(F32), 0.0).then_inc(cleared, 1)

            def norm(m, _):
                pool.wait_ge(gvar_ready, m + 1)
                nc.gpsimd.tensor_tensor(rstd[:, m, :], gvar[:, m, :], minus_half[:, :], ALU.pow).then_inc(rstd_ready, 1)

            def split(m, _):
                l, p = where(m)
                if m >= PAIRS:
                    pool.wait_ge(off_parts, 4 * (m - 1))
                pool.wait_ge(cleared, 3)
                pool.wait_ge(x16_ready, 2 * m + 1)
                nc.gpsimd.tensor_copy(xpad_v[:, 2 * p, 1:H + 1, 1:W + 1],
                                      xh[:, 2 * p, :].rearrange("p (h w) -> p h w", h=H)).then_inc(xpad0, 1)

            def column_tents(m, a):
                ky, kx, bb = a
                if ky not in POOL_KY:
                    return
                pool.wait_ge(tx_abs, 18 * m + 6 * ky + 2 * kx + bb + 1)
                v = tx[:, ky % TX_SLOTS, kx, HW * bb:HW * (bb + 1)]
                nc.gpsimd.tensor_scalar(v, v, 1.0, 0.0, ALU.min, ALU.max).then_inc(tx_pool, 1)

            def final_scale(m, _):
                l, p = where(m)
                pool.wait_ge(fin_var, p + 1)
                nc.gpsimd.tensor_tensor(fin[:, p, 5:6], fin[:, p, 4:5], minus_half[:, 0:1], ALU.pow).then_inc(fin_rstd, 1)

            part = {"norm": norm, "split": split, "tx": column_tents, "final scale": final_scale}
            pool.wait_ge(cleared, 1)
            for name, m, a in before() + [x for m in range(STAGES) for at in during(m) for x in at]:
                if name in part:
                    part[name](m, a)
            final_scale(STAGES - 1, 0)

        @block.scalar
        def _(act):
            act.dma_start(w_raw[0][0][:, :], w_off[0]).then_inc(w_here[0][0], 16)
            act.dma_start(vec[:, :], vecs).then_inc(vec_here, 16)
            act.dma_start(w_raw[0][1][:, :], w_def[0]).then_inc(w_here[0][1], 16)
            act.dma_start(half[:, :], c_half).then_inc(half_here, 16)
            act.wait_ge(vec_here, 16)

            def weights(l, _):
                wait_full(act, ("weights", l, 0))
                v = tbuf(("weights", l, 0))[:, 0:TAPS * 64].rearrange("p (t o) -> p t o", t=TAPS)
                nc.scalar.activation(w_off16[l][:, :, 0:32], v[:, :, 0:32], ACT.Copy).then_inc(wt_high, 1)
                wait_full(act, ("weights", l, 1))
                nc.scalar.activation(w_hi[l][:, :], tbuf(("weights", l, 1))[:, 0:TAPS * C], ACT.Copy).then_inc(wt_high, 1)

            def norm(m, _):
                l, p = where(m)
                if m >= PAIRS:
                    act.wait_ge(z_ready, 2 * CHUNKS * (m - 1))
                    act.wait_ge(xpad0, m - 1)
                for bb in range(2):
                    act.wait_ge(xn_ready, 2 * m + bb + 1)
                    nc.scalar.activation(xh[:, 2 * p + bb, :], xn[:, bb, :], ACT.Copy).then_inc(xh_ready, 1)

            def split(m, _):
                l, p = where(m)
                act.wait_ge(cleared, 3)
                act.wait_ge(x16_ready, 2 * m + 2)
                nc.scalar.activation(xpad_v[:, 2 * p + 1, 1:H + 1, 1:W + 1],
                                     xh[:, 2 * p + 1, :].rearrange("p (h w) -> p h w", h=H), ACT.Copy).then_inc(xpad1, 1)

            def offsets(m, _):
                l, p = where(m)
                wait_full(act, ("conv", m, 0))
                v = banks(tbuf(("conv", m, 0)))
                if m:
                    act.wait_ge(pos_ready, 2 * m)
                    act.wait_ge(omax_ready, 3 * m)
                if m > PAIRS:
                    act.wait_ge(msk_ready, 2 * (m - PAIRS))
                for bb in range(2):
                    for i, dst in enumerate((off_a, off_b)):
                        r = slice(64 * bb + LO * i, 64 * bb + LO * i + OFF)
                        nc.scalar.activation(halves(dst[:, bb, :]), v[r], ACT.Identity, scale=w_max[r, 2 * l:2 * l + 1],
                                             bias=vec[r, l:l + 1] if i == 0 else 0.0).then_inc(off_parts, 1)
                act.wait_ge(off_parts, 4 * m + 4)
                act.sem_inc(free_of(("conv", m, 0)), 1)

            def position(m, _):
                l, p = where(m)
                if m >= PAIRS:
                    act.wait_ge(tx_abs, 18 * (m - 1))
                for bb in range(2):
                    act.wait_ge(off_sum, 2 * m + bb + 1)
                    act.wait_ge(cleared, 2)
                    nc.scalar.activation(pos[0:OFF, 2 * p + bb, :], off_b[:, bb, :], ACT.Copy).then_inc(pos_high, 1)
                if l:
                    act.wait_ge(omax_ready, 3 * m + 2)
                    act.wait_ge(cleared, 5)
                    for bb in range(2):
                        nc.scalar.activation(off_a[:, bb, :], off_a[:, bb, :], ACT.Sigmoid).then_inc(sig_ready, 1)
                    for bb in range(2):
                        act.wait_ge(sig_ready, 2 * (m - PAIRS) + bb + 1)
                        nc.scalar.activation(msk[0:OFF, 2 * p + bb, :], off_a[:, bb, :], ACT.Copy).then_inc(msk_high, 1)

            def z_out(m, i):
                l, p = where(m)
                j, bb = divmod(i, 2)
                q = pixels(j)
                wait_full(act, ("z", m, i))
                if m >= PAIRS:
                    act.wait_ge(s_used, NSTEPS * (m - 1))
                nc.scalar.activation(halves(z[0:q, 2 * p + bb, j, :]), banks(tbuf(("z", m, i))[0:q]), ACT.Copy)\
                    .then_inc(z_ready, 1)
                act.wait_ge(z_ready, 2 * CHUNKS * m + i + 1)
                act.sem_inc(free_of(("z", m, i)), 1)

            def y_tents(m, j):
                n = CHUNKS * m + j
                nw = (wide(j)[1] - wide(j)[0]) * W
                wait_full(act, ("y", m, j))
                if n >= 2:
                    act.wait_ge(yt_ready, n - 1)
                nc.scalar.activation(ya[:, n % 2, :, 0:nw], halves(tbuf(("y", m, j))[0:YROWS])[:, :, 0:nw], ACT.Abs)\
                    .then_inc(ya_ready, 1)
                act.wait_ge(ya_ready, n + 1)
                act.sem_inc(free_of(("y", m, j)), 1)
                if n >= 2:
                    act.wait_ge(ytent_ready, n - 1)
                nc.scalar.activation(yt[:, n % 2, :, 0:nw], ya[:, n % 2, :, 0:nw], ACT.Relu, scale=-1.0, bias=1.0)\
                    .then_inc(yt_ready, 1)

            def y_end(m, j):
                l, p = where(m)
                n = CHUNKS * m + j
                nw = (wide(j)[1] - wide(j)[0]) * W
                if l:
                    act.wait_ge(ym_ready, n - CHUNKS * PAIRS + 1)
                else:
                    act.wait_ge(yt_ready, n + 1)
                nc.scalar.activation(yh[:, n % 2, :, 0:nw], (ym if l else yt)[:, n % 2, :, 0:nw], ACT.Copy)\
                    .then_inc(yh_ready, 1)

            def column_tents(m, a):
                ky, kx, bb = a
                unit, n = 3 * m + ky, 18 * m + 6 * ky + 2 * kx + bb
                if unit >= TX_SLOTS:
                    act.wait_ge(s_ready, 2 * CHUNKS * (unit - TX_SLOTS + 1))
                wait_full(act, ("tx", m, a))
                v = tx[:, ky % TX_SLOTS, kx, HW * bb:HW * (bb + 1)]
                nc.scalar.activation(halves(v), banks(tbuf(("tx", m, a))[0:ROWS * W]), ACT.Abs).then_inc(tx_abs, 1)
                act.wait_ge(tx_abs, n + 1)
                act.sem_inc(free_of(("tx", m, a)), 1)
                if ky not in POOL_KY:
                    nc.scalar.activation(v, v, ACT.Relu, scale=-1.0, bias=1.0).then_inc(tx_act, 1)

            def sums_out(m):
                l, p = where(m)
                act.wait_ge(acc_full, m + 1)
                if m >= PAIRS:
                    act.wait_ge(x_mid, 4 * (p + 1))
                nc.scalar.activation(halves(y[:, p, :]), acc[:, :, 0:HALF], ACT.Identity,
                                     scale=w_neg[:, l:l + 1], bias=vec[:, 2 + l:3 + l]).then_inc(y_ready, 1)
                act.wait_ge(y_ready, m + 1)
                act.sem_inc(acc_free, 1)

            def general(m):
                l, p = where(m)
                na, nd, np_ = g_steps(l)
                with act.Fori(0, TAPS) as k:
                    for bb in range(2):
                        it = 2 * k + bb
                        b = 2 * p + bb
                        act.wait_ge(g_pe[m], np_ * it + 1)
                        nc.scalar.activation(g_pos, pos[0:KPOS, b, :], ACT.Copy).then_inc(g_act[m], 1)
                        nc.scalar.activation(g_ex, ex[0:KPOS, bass.ds(k, 1), :], ACT.Copy).then_inc(g_act[m], 1)
                        nc.scalar.activation(g_ef, ef[0:KPOS, bass.ds(k, 1), :], ACT.Copy).then_inc(g_act[m], 1)
                        zf = z[:, b, :, :].rearrange("q j (k o) -> q j k o", k=TAPS)
                        nc.scalar.activation(g_z[:, 0:4 * C].rearrange("q (j o) -> q j o", j=4),
                                             zf[:, 0:4, bass.ds(k, 1), :], ACT.Copy).then_inc(g_act[m], 1)
                        nc.scalar.activation(g_z[0:pixels(4), 4 * C:5 * C], zf[0:pixels(4), 4, bass.ds(k, 1), :],
                                             ACT.Copy).then_inc(g_act[m], 1)
                        if l:
                            nc.scalar.activation(g_msk, msk[:, b, :], ACT.Copy).then_inc(g_act[m], 1)
                            nc.scalar.activation(g_em, em[0:KMASK, bass.ds(k, 1), :], ACT.Copy).then_inc(g_act[m], 1)
                        act.wait_ge(g_pe[m], np_ * it + 2)
                        nc.scalar.activation(halves(g_xt), banks(tb[0:ROWS * W, 0, :]), ACT.Abs).then_inc(g_act[m], 1)
                        act.wait_ge(g_act[m], na * it + 6 + 2 * l)
                        nc.scalar.activation(g_xt, g_xt, ACT.Relu, scale=-1.0, bias=1.0).then_inc(g_act[m], 1)
                        for j in range(CHUNKS):
                            act.wait_ge(g_pe[m], np_ * it + 3 + 2 * j)
                            nc.scalar.activation(halves(g_yt), banks(tb[0:ROWS * W, 1, :]), ACT.Abs,
                                                 bias=full[0:ROWS * W, 514 + j:515 + j]).then_inc(g_act[m], 1)
                act.wait_ge(g_sum[m], 1)
                nc.scalar.activation(halves(y[:, p, :]), acc[:, :, 0:HALF], ACT.Identity,
                                     scale=w_neg[:, l:l + 1], bias=vec[:, 2 + l:3 + l]).then_inc(g_out[m], 1)
                act.wait_ge(g_out[m], 1)

            def final_out(m, _):
                l, p = where(m)
                act.wait_ge(fin_ready, p + 1)
                nc.scalar.activation(res[:, p, :], y[:, p, :], ACT.Relu, scale=fin[:, p, 6:7], bias=fin[:, p, 7:8])\
                    .then_inc(relu_ready, 1)

            part = {"weights": weights, "norm": norm, "split": split, "offsets": offsets, "position": position,
                    "z": z_out, "y": y_tents, "y end": y_end, "tx": column_tents, "final out": final_out}
            for name, n, a in before():
                if name in part:
                    part[name](n, a)
            for m in range(STAGES):
                for at in during(m):
                    for name, n, a in at:
                        if name in part:
                            part[name](n, a)
                sums_out(m)
                with act.If(far(act, m)):
                    general(m)
            final_out(STAGES - 1, 0)

        @block.vector
        def _(dve):
            count = [0]

            def then(ins):
                count[0] += 1
                ins.then_inc(dve_c, 1)
                dve.wait_ge(dve_c, count[0])

            def weights(l, _):
                for i in range(2):
                    m = slice(2 * l + i, 2 * l + i + 1)
                    dve.wait_ge(w_here[l][i], 16)
                    then(nc.vector.tensor_reduce(w_max[:, m], w_raw[l][i][:, :], axis=AX.X, op=ALU.max,
                                                 apply_absolute_value=True))
                    then(nc.vector.tensor_scalar(w_max[:, m], w_max[:, m], 1e-30, None, ALU.max))
                    then(nc.vector.reciprocal(w_inv[:, m], w_max[:, m]))
                    if l:
                        dve.wait_ge(wt_high, 2 * l)
                    for d in range(2):
                        nc.vector.tensor_scalar(w_unit[i][:, :, d, :],
                                                w_raw[l][i][:, :].rearrange("o (t c) -> o t c", t=TAPS),
                                                w_inv[:, m], None, ALU.mult).then_inc(w_scaled, 1)
                then(nc.vector.tensor_scalar(w_neg[:, l:l + 1], w_max[:, 2 * l + 1:2 * l + 2], -1.0, None, ALU.mult))
                name = ("weights", l, 0)
                dve.wait_ge(wt_high, 2 * l + 1)
                v = tbuf(name)[:, 0:TAPS * 64].rearrange("p (t o) -> p t o", t=TAPS)[:, :, 32:64]
                nc.vector.tensor_tensor(w_off16[l][:, :, 32:64], v, w_off16[l][:, :, 0:32], ALU.subtract)\
                    .then_inc(wt_done, 1)
                dve.wait_ge(wt_done, 2 * l + 1)
                dve.sem_inc(free_of(name), 1)
                name = ("weights", l, 1)
                dve.wait_ge(wt_high, 2 * l + 2)
                nc.vector.tensor_tensor(w_lo[l][:, :], tbuf(name)[:, 0:TAPS * C], w_hi[l][:, :], ALU.subtract)\
                    .then_inc(wt_done, 1)
                dve.wait_ge(wt_done, 2 * l + 2)
                dve.sem_inc(free_of(name), 1)

            def stats(m, _):
                l, p = where(m)
                for bb in range(2):
                    r = slice(64 * bb, 64 * bb + 64)
                    for d in (1 - bb, bb):
                        if l:
                            dve.wait_ge(y_ready, p + 1)
                            nc.vector.tensor_tensor(x_l[64 * d:64 * d + 64, 2 * p + bb, :], y[r, p, :],
                                                    x_l[r, 2 * p + bb, :], ALU.add).then_inc(x_mid, 1)
                if l:
                    dve.wait_ge(x_mid, 4 * p + 4)
                for bb in range(2):
                    dve.wait_ge(x_here[2 * p + bb], 32)
                    for i in range(2):
                        nc.vector.bn_stats(bn[:, m, bb, i, :], x_l[:, 2 * p + bb, HALF * i:HALF * (i + 1)]).then_inc(dve_c, 1)
                count[0] += 4
                dve.wait_ge(dve_c, count[0])
                for bb in range(2):
                    nc.vector.bn_aggr(chan[:, m, :, bb], bn[:, m, bb, :, :]).then_inc(stats_ready, 1)

            def norm(m, _):
                l, p = where(m)
                wait_full(dve, ("norm", m, 0))
                then(nc.vector.tensor_copy(group[:, m, :, :],
                                           tbuf(("norm", m, 0))[:, 0:6].rearrange("p (a b) -> p a b", a=3)))
                dve.sem_inc(free_of(("norm", m, 0)), 1)
                then(nc.vector.tensor_tensor(gsq[:, m, :], group[:, m, 2, :], group[:, m, 2, :], ALU.mult))
                then(nc.vector.tensor_tensor(gsq[:, m, :], gsq[:, m, :], group[:, m, 1, :], ALU.add))
                nc.vector.tensor_scalar(gvar[:, m, :], gsq[:, m, :], GN_EPS, None, ALU.add).then_inc(gvar_ready, 1)
                dve.wait_ge(rstd_ready, m + 1)
                if m:
                    dve.wait_ge(xh_ready, 2 * m)
                    dve.wait_ge(x16_ready, 2 * m)
                for bb in range(2):
                    nc.vector.tensor_scalar(xn[:, bb, :], x_l[:, 2 * p + bb, :], group[:, m, 0, bb:bb + 1],
                                            rstd[:, m, bb:bb + 1], ALU.subtract, ALU.mult).then_inc(xn_ready, 1)

            def split(m, _):
                l, p = where(m)
                for bb in range(2):
                    dve.wait_ge(xn_ready, 2 * m + bb + 1)
                    dve.wait_ge(xh_ready, 2 * m + bb + 1)
                    nc.vector.scalar_tensor_tensor(out=xh[:, 2 * p + bb, :], in0=xh[:, 2 * p + bb, :], scalar=low_c,
                                                   in1=xn[:, bb, :], op0=ALU.mult, op1=ALU.add).then_inc(x16_ready, 1)

            def offsets(m, _):
                for bb in range(2):
                    dve.wait_ge(off_parts, 4 * m + 2 * bb + 2)
                    then(nc.vector.tensor_tensor(off_a[:, bb, :], off_a[:, bb, :], off_b[:, bb, :], ALU.add))
                    nc.vector.tensor_scalar(off_b[:, bb, :], off_a[:, bb, :], -BIG, BIG, ALU.max, ALU.min)\
                        .then_inc(off_sum, 1)
                    nc.vector.tensor_reduce(omax[0:NOFF, m, bb:bb + 1], off_a[0:NOFF, bb, :], axis=AX.X, op=ALU.max,
                                            apply_absolute_value=True).then_inc(omax_ready, 1)
                dve.wait_ge(omax_ready, 3 * m + 2)
                nc.vector.tensor_reduce(omax1[0:NOFF, m:m + 1], omax[0:NOFF, m, :], axis=AX.X, op=ALU.max)\
                    .then_inc(omax_ready, 1)

            def position(m, _):
                l, p = where(m)
                for bb in range(2):
                    b = 2 * p + bb
                    dve.wait_ge(pos_high, 2 * m + bb + 1)
                    nc.vector.tensor_tensor(pos[LO:LO + OFF, b, :], off_b[:, bb, :], pos[0:OFF, b, :], ALU.subtract)\
                        .then_inc(pos_ready, 1)
                if l:
                    for bb in range(2):
                        b = 2 * p + bb
                        dve.wait_ge(msk_high, 2 * (m - PAIRS) + bb + 1)
                        nc.vector.tensor_tensor(msk[LO:LO + OFF, b, :], off_a[:, bb, :], msk[0:OFF, b, :], ALU.subtract)\
                            .then_inc(msk_ready, 1)

            def find_far(m, _):
                wait_full(dve, ("flag", m, 0))
                then(nc.vector.tensor_reduce(oall[:, m:m + 1], tbuf(("flag", m, 0))[0:1, 0:NOFF], axis=AX.X, op=ALU.max))
                dve.sem_inc(free_of(("flag", m, 0)), 1)
                nc.vector.tensor_scalar(flag[:, m:m + 1], oall[:, m:m + 1], float(REACH), None, ALU.is_gt)\
                    .then_inc(flag_ready, 1)

            def y_tents(m, j):
                if m < PAIRS:
                    return
                n = CHUNKS * m + j
                nw = (wide(j)[1] - wide(j)[0]) * W
                wait_full(dve, ("mask", m, j))
                dve.wait_ge(yt_ready, n + 1)
                nc.vector.tensor_tensor(ym[:, n % 2, :, 0:nw], halves(tbuf(("mask", m, j))[0:YROWS])[:, :, 0:nw],
                                        yt[:, n % 2, :, 0:nw], ALU.mult).then_inc(ym_ready, 1)
                dve.wait_ge(ym_ready, n - CHUNKS * PAIRS + 1)
                dve.sem_inc(free_of(("mask", m, j)), 1)

            def y_end(m, j):
                l, p = where(m)
                n = CHUNKS * m + j
                nw = (wide(j)[1] - wide(j)[0]) * W
                dve.wait_ge(yh_ready, n + 1)
                nc.vector.scalar_tensor_tensor(
                    out=ytent[:, 2 * p:2 * p + 2, WIDE_AT[j]:WIDE_AT[j] + nw], in0=yh[:, n % 2, :, 0:nw],
                    scalar=low_y, in1=(ym if l else yt)[:, n % 2, :, 0:nw], op0=ALU.mult, op1=ALU.add)\
                    .then_inc(ytent_ready, 1)

            def sampling(m, g):
                ky, j = STEPS[g]
                q = pixels(j)
                r0, r1 = band(j, ky)
                nb = (r1 - r0) * W
                tents_wait(dve, m, ky)
                for bb in range(2):
                    i = 2 * g + bb
                    n = ITEMS * m + i
                    name = ("item", m, i)
                    if n >= S_SLOTS:
                        dve.wait_ge(s_used, n // 2 - S_SLOTS // 2 + 1)
                    wait_full(dve, name)
                    nc.vector.scalar_tensor_tensor(
                        out=s[0:q, n % S_SLOTS, :, 0:nb],
                        in0=tx[0:q, ky % TX_SLOTS, :, HW * bb + W * r0:HW * bb + W * r1],
                        scalar=1.0 if ky in POOL_KY else -1.0,
                        in1=tbuf(name)[0:q, 0:3 * SLOT].rearrange("p (k c) -> p k c", k=3)[:, :, 0:nb],
                        op0=ALU.subtract if ky in POOL_KY else ALU.mult, op1=ALU.mult).then_inc(s_ready, 1)
                    dve.wait_ge(s_ready, n + 1)
                    dve.sem_inc(free_of(name), 1)

            def general(m):
                l, p = where(m)
                na, nd, np_ = g_steps(l)
                dve.wait_ge(y_ready, m + 1)
                dve.sem_inc(g_dve[m], 1)
                with dve.Fori(0, TAPS) as k:
                    for bb in range(2):
                        it = 2 * k + bb
                        for j in range(CHUNKS):
                            done = nd * it + (2 + l) * j + 1
                            dve.wait_ge(g_act[m], na * it + 8 + 2 * l + j)
                            nc.vector.tensor_scalar(g_yt, g_yt, 1.0, 1.0, ALU.min, ALU.subtract).then_inc(g_dve[m], 1)
                            dve.wait_ge(g_dve[m], done + 1)
                            nc.vector.tensor_tensor(g_s, g_yt, g_xt, ALU.mult).then_inc(g_dve[m], 1)
                            if l:
                                dve.wait_ge(g_dve[m], done + 2)
                                nc.vector.tensor_tensor(halves(g_s), banks(tb[0:ROWS * W, 2, :]), halves(g_s),
                                                        ALU.mult).then_inc(g_dve[m], 1)
                dve.wait_ge(g_out[m], 1)

            def final_mean(m, _):
                l, p = where(m)
                dve.wait_ge(y_ready, m + 1)
                for i in range(2):
                    nc.vector.bn_stats(bn[:, p, 0, i, :], y[:, p, HALF * i:HALF * (i + 1)]).then_inc(dve_c, 1)
                count[0] += 2
                dve.wait_ge(dve_c, count[0])
                nc.vector.bn_aggr(fin[:, p, 0:2], bn[:, p, 0, :, :]).then_inc(fin_stats, 1)

            def final_spread(m, _):
                l, p = where(m)
                name = ("final mean", m, 0)
                wait_full(dve, name)
                then(nc.vector.tensor_copy(fin[:, p, 2:4], tbuf(name)[:, 0:2]))
                dve.sem_inc(free_of(name), 1)
                then(nc.vector.tensor_tensor(fin[:, p, 4:5], fin[:, p, 0:1], fin[:, p, 2:3], ALU.subtract))
                nc.vector.tensor_tensor(fin[:, p, 5:6], fin[:, p, 4:5], fin[:, p, 4:5], ALU.mult).then_inc(fin_stats, 1)

            def final_scale(m, _):
                l, p = where(m)
                name = ("final variance", m, 0)
                wait_full(dve, name)
                then(nc.vector.tensor_tensor(fin[:, p, 3:4], tbuf(name)[:, 0:1], fin[:, p, 3:4], ALU.add))
                dve.sem_inc(free_of(name), 1)
                nc.vector.tensor_scalar(fin[:, p, 4:5], fin[:, p, 3:4], GN_EPS, None, ALU.add).then_inc(fin_var, 1)
                dve.wait_ge(fin_rstd, p + 1)
                then(nc.vector.tensor_scalar(fin[:, p, 6:7], fin[:, p, 5:6], vec[:, 4:5], None, ALU.mult))
                then(nc.vector.tensor_tensor(fin[:, p, 4:5], fin[:, p, 2:3], fin[:, p, 6:7], ALU.mult))
                nc.vector.tensor_scalar(fin[:, p, 7:8], fin[:, p, 4:5], -1.0, vec[:, 5:6], ALU.mult, ALU.add)\
                    .then_inc(fin_ready, 1)

            def final_out(m, _):
                l, p = where(m)
                dve.wait_ge(relu_ready, p + 1)
                for bb in range(2):
                    r = slice(64 * bb, 64 * bb + 64)
                    nc.vector.tensor_tensor(res[r, p, :], res[r, p, :], x_l[r, 2 * p + bb, :], ALU.add).then_inc(res_ready, 1)

            part = {"weights": weights, "stats": stats, "norm": norm, "split": split, "offsets": offsets,
                    "position": position, "flag": find_far, "y": y_tents, "y end": y_end, "final mean": final_mean,
                    "final spread": final_spread, "final scale": final_scale, "final out": final_out}
            dve.wait_ge(full_here, 16)
            dve.wait_ge(vec_here, 16)
            for name, n, a in before():
                if name in part:
                    part[name](n, a)
            for m in range(STAGES):
                sampling(m, 0)
                for g, at in enumerate(during(m)):
                    if g + 1 < NSTEPS:
                        sampling(m, g + 1)
                    for name, n, a in at:
                        if name in part:
                            part[name](n, a)
                with dve.If(far(dve, m)):
                    general(m)
            final_mean(STAGES - 1, 0)
            final_spread(STAGES - 1, 0)
            final_scale(STAGES - 1, 0)
            final_out(STAGES - 1, 0)

        @block.tensor
        def _(pe):
            mm = nc.tensor.matmul

            def take(name):
                n = JOB[name]
                if n >= T_BUFS:
                    pe.wait_ge(t_free[n % T_BUFS], n // T_BUFS)
                return t_full[n % T_BUFS]

            def weights(l, _):
                for i in range(2):
                    name = ("weights", l, i)
                    pe.wait_ge(w_scaled, 4 * l + 2 * i + 2)
                    full_sem = take(name)
                    for t in range(TAPS):
                        last = nc.tensor.transpose(tbuf(name)[:, 64 * t:64 * t + 64], w_unit[i][0:64, t, :, :],
                                                   ident[0:64, 0:64])
                    last.then_inc(full_sem, 1)

            def norm(m, _):
                name = ("norm", m, 0)
                pe.wait_ge(stats_ready, 2 * (m + 1))
                full_sem = take(name)
                mm(tbuf(name)[:, 0:4], pair_m, chan[:, m, :, :], start=True, stop=True)
                mm(tbuf(name)[:, 4:6], diff_m, chan[:, m, 0, :], start=True, stop=True).then_inc(full_sem, 1)

            def conv(m, _):
                l, p = where(m)
                name = ("conv", m, 0)
                pe.wait_ge(wt_done, 2 * l + 1)
                pe.wait_ge(xpad0, m + 1)
                pe.wait_ge(xpad1, m + 1)
                full_sem = take(name)
                for t in range(TAPS):
                    ty, tx_ = divmod(t, 3)
                    for hf in range(2):
                        for bb in range(2):
                            last = mm(tbuf(name)[64 * bb:64 * bb + 64, BANK * hf:BANK * hf + HALF], w_off16[l][:, t, :],
                                      xpad_v[:, 2 * p + bb, 12 * hf + ty:12 * hf + ty + 12, tx_:tx_ + W],
                                      start=t == 0, stop=t == TAPS - 1)
                last.then_inc(full_sem, 1)

            def z_products(m, i):
                l, p = where(m)
                j, bb = divmod(i, 2)
                q = pixels(j)
                name = ("z", m, i)
                pe.wait_ge(wt_done, 2 * l + 2)
                pe.wait_ge(x16_ready, 2 * m + bb + 1)
                full_sem = take(name)
                for hf in range(2):
                    for i_part, wp in enumerate((w_hi[l], w_lo[l])):
                        last = mm(tbuf(name)[0:q, BANK * hf:BANK * hf + HALF],
                                  xh[:, 2 * p + bb, ROWS * W * j:ROWS * W * j + q], wp[:, HALF * hf:HALF * (hf + 1)],
                                  start=i_part == 0, stop=i_part == 1)
                last.then_inc(full_sem, 1)

            def y_distances(m, j):
                l, p = where(m)
                r0, r1 = wide(j)
                pe.wait_ge(half_here, 16)
                pe.wait_ge(pos_here, 16)
                pe.wait_ge(pos_ready, 2 * (m + 1))
                full_sem = take(("y", m, j))
                for bb in range(2):
                    last = mm(tbuf(("y", m, j))[0:YROWS, BANK * bb:BANK * bb + (r1 - r0) * W], ey[0:KPOS, j, :],
                              pos[0:KPOS, 2 * p + bb, W * r0:W * r1], start=True, stop=True)
                last.then_inc(full_sem, 1)
                if l:
                    pe.wait_ge(msk_ready, 2 * (m - PAIRS + 1))
                    full_sem = take(("mask", m, j))
                    for bb in range(2):
                        last = mm(tbuf(("mask", m, j))[0:YROWS, BANK * bb:BANK * bb + (r1 - r0) * W], my[0:KMASK, 0, :],
                                  msk[:, 2 * p + bb, W * r0:W * r1], start=True, stop=True)
                    last.then_inc(full_sem, 1)

            def largest_offset(m, _):
                name = ("flag", m, 0)
                pe.wait_ge(omax_ready, 3 * (m + 1))
                full_sem = take(name)
                nc.tensor.transpose(tbuf(name)[0:1, 0:NOFF], omax1[0:NOFF, m:m + 1], ident[0:NOFF, 0:NOFF])\
                    .then_inc(full_sem, 1)

            def x_distances(m, a):
                l, p = where(m)
                ky, kx, bb = a
                name = ("tx", m, a)
                full_sem = take(name)
                for hf in range(2):
                    last = mm(tbuf(name)[0:ROWS * W, BANK * hf:BANK * hf + HALF], ex[0:KPOS, 3 * ky + kx, :],
                              pos[0:KPOS, 2 * p + bb, HALF * hf:HALF * (hf + 1)], start=True, stop=True)
                last.then_inc(full_sem, 1)

            def spread_rows(m, g):
                l, p = where(m)
                ky, j = STEPS[g]
                r0, r1 = band(j, ky)
                at = WIDE_AT[j] + W * (r0 - wide(j)[0])
                pe.wait_ge(ytent_ready, CHUNKS * m + j + 1)
                for bb in range(2):
                    name = ("item", m, 2 * g + bb)
                    full_sem = take(name)
                    for kx in range(3):
                        last = mm(tbuf(name)[0:pixels(j), SLOT * kx:SLOT * kx + W * (r1 - r0)],
                                  sel[0:YROWS, 3 * ky + kx, 0:pixels(j)],
                                  ytent[:, 2 * p + bb, at:at + W * (r1 - r0)], start=True, stop=True)
                    last.then_inc(full_sem, 1)

            def clear_acc():
                for hf in range(2):
                    mm(acc[:, hf, 0:HALF], zeros[0:1, 0:128], zeros[0:1, 0:HALF], start=True, stop=False,
                       skip_group_check=True)

            def products(m, g):
                l, p = where(m)
                ky, j = STEPS[g]
                q = pixels(j)
                r0, r1 = band(j, ky)
                if g == 0:
                    pe.wait_ge(cleared, 4)
                    if m:
                        pe.wait_ge(acc_free, m)
                    clear_acc()
                pe.wait_ge(z_ready, 2 * CHUNKS * m + 2 * j + 2)
                pe.wait_ge(s_ready, ITEMS * m + 2 * g + 2)
                for kx in range(3):
                    k = 3 * ky + kx
                    for hf in range(2):
                        a, b = max(r0, 12 * hf), min(r1, 12 * hf + 12)
                        if a >= b:
                            continue
                        for bb in range(2):
                            n = ITEMS * m + 2 * g + bb
                            last = mm(acc[64 * bb:64 * bb + 64, hf, W * (a - 12 * hf):W * (b - 12 * hf)],
                                      z[0:q, 2 * p + bb, j, 64 * k:64 * k + 64],
                                      s[0:q, n % S_SLOTS, kx, W * (a - r0):W * (b - r0)],
                                      start=False, stop=g == NSTEPS - 1 and kx == 2, skip_group_check=True)
                last.then_inc(s_used, 1)
                if g == NSTEPS - 1:
                    pe.wait_ge(s_used, NSTEPS * (m + 1))
                    pe.sem_inc(acc_full, 1)

            def general(m):
                l, p = where(m)
                na, nd, np_ = g_steps(l)
                pe.wait_ge(y_ready, m + 1)
                at_end = during(m)[-1]
                issued = max(JOB[x] for x in JOB if x[0] == "item" and x[1] == m)
                issued = max([issued] + [JOB[x] for x in JOB if m + 1 < STAGES and JOB[x] < JOB["item", m + 1, 0]])
                for i in range(T_BUFS):
                    pe.wait_ge(t_free[i], (issued - i) // T_BUFS + 1)
                clear_acc()
                pe.sem_inc(g_pe[m], 1)
                with pe.Fori(0, TAPS) as k:
                    for bb in range(2):
                        it = 2 * k + bb
                        pe.wait_ge(g_act[m], na * it + 5 + 2 * l)
                        for hf in range(2):
                            last = mm(tb[0:ROWS * W, 0, BANK * hf:BANK * hf + HALF], g_ex,
                                      g_pos[:, HALF * hf:HALF * (hf + 1)], start=True, stop=True)
                        last.then_inc(g_pe[m], 1)
                        for j in range(CHUNKS):
                            q = pixels(j)
                            pe.wait_ge(g_dve[m], nd * it + (2 + l) * j + 1)
                            for hf in range(2):
                                c = slice(HALF * hf, HALF * (hf + 1))
                                last = mm(tb[0:ROWS * W, 1, BANK * hf:BANK * hf + HALF], g_ef,
                                          g_pos[:, c], start=True, stop=True)
                                if l:
                                    last = mm(tb[0:ROWS * W, 2, BANK * hf:BANK * hf + HALF], g_em,
                                              g_msk[:, c], start=True, stop=True)
                            last.then_inc(g_pe[m], 1)
                            pe.wait_ge(g_dve[m], nd * it + (2 + l) * (j + 1) + 1)
                            for hf in range(2):
                                last = mm(acc[64 * bb:64 * bb + 64, hf, 0:HALF], g_z[0:q, C * j:C * (j + 1)],
                                          g_s[0:q, HALF * hf:HALF * (hf + 1)], start=False, stop=False,
                                          skip_group_check=True)
                            last.then_inc(g_pe[m], 1)
                pe.wait_ge(g_pe[m], np_ * 2 * TAPS + 1)
                pe.sem_inc(g_sum[m], 1)
                pe.wait_ge(g_out[m], 1)

            def final_mean(m, _):
                l, p = where(m)
                pe.wait_ge(fin_stats, 2 * p + 1)
                full_sem = take(("final mean", m, 0))
                mm(tbuf(("final mean", m, 0))[:, 0:2], block_m, fin[:, p, 0:2], start=True, stop=True).then_inc(full_sem, 1)

            def final_variance(m, _):
                l, p = where(m)
                pe.wait_ge(fin_stats, 2 * p + 2)
                full_sem = take(("final variance", m, 0))
                mm(tbuf(("final variance", m, 0))[:, 0:1], block_m, fin[:, p, 5:6], start=True, stop=True)\
                    .then_inc(full_sem, 1)

            part = {"weights": weights, "norm": norm, "conv": conv, "z": z_products, "y": y_distances,
                    "flag": largest_offset, "final mean": final_mean, "final variance": final_variance}
            pe.wait_ge(full_here, 16)
            for name, n, a in before():
                if name == "tx":
                    x_distances(n, a)
                elif name in part:
                    part[name](n, a)
            for m in range(STAGES):
                spread_rows(m, 0)
                for g, at in enumerate(during(m)):
                    for name, n, a in at:
                        if name == "tx":
                            x_distances(n, a)
                    if g + 1 < NSTEPS:
                        spread_rows(m, g + 1)
                    products(m, g)
                    for name, n, a in at:
                        if name in part:
                            part[name](n, a)
                with pe.If(far(pe, m)):
                    general(m)
            final_mean(STAGES - 1, 0)
            final_variance(STAGES - 1, 0)


def kernel(x, L0_conv_w_off, L0_conv_b_off, L0_conv_w_def, L0_conv_b_def,
           L1_conv_w_off, L1_conv_b_off, L1_conv_w, L1_conv_b, L1_conv_gamma, L1_conv_beta):
    import concourse.bacc as bacc
    from concourse.bass_utils import run_bass_kernel_spmd

    def off_rows(a):
        a = np.asarray(a)
        return np.tile(np.pad(a, [(0, 32 - a.shape[0])] + [(0, 0)] * (a.ndim - 1)), [4] + [1] * (a.ndim - 1))

    def taps(w):
        w = np.asarray(w)
        return w.transpose(0, 2, 3, 1).reshape(w.shape[0], TAPS * C)

    def twice(a):
        a = np.asarray(a)
        return np.concatenate([a, a], 0)

    half, full, pos = constants()
    vecs = np.stack([off_rows(L0_conv_b_off), off_rows(L1_conv_b_off), twice(L0_conv_b_def), twice(L1_conv_b),
                     twice(L1_conv_gamma), twice(L1_conv_beta)], 1)
    arrays = {
        "x": np.ascontiguousarray(np.asarray(x).reshape(B, C, HW)),
        "w_off": np.ascontiguousarray(np.stack([off_rows(taps(L0_conv_w_off)), off_rows(taps(L1_conv_w_off))])),
        "w_def": np.ascontiguousarray(np.stack([twice(taps(L0_conv_w_def)), twice(taps(L1_conv_w))])),
        "vecs": np.ascontiguousarray(vecs), "c_half": half, "c_full": full, "c_pos": np.ascontiguousarray(pos),
    }
    nc = bacc.Bacc("TRN2", target_bir_lowering=False, num_devices=1)
    args = {n: nc.dram_tensor(n, a.shape, mybir.dt.from_np(a.dtype), kind="ExternalInput").ap() for n, a in arrays.items()}
    out = nc.dram_tensor("out", (B, C, HW), F32, kind="ExternalOutput").ap()
    build(nc, out=out, **args)
    r = run_bass_kernel_spmd(nc, [arrays], core_ids=[0])
    return r.results[0]["out"].reshape(B, C, H, W)
```

```python
from contextlib import ExitStack

import numpy as np

import concourse.bass as bass
from concourse import mybir

F32, F16, I32 = mybir.dt.float32, mybir.dt.float16, mybir.dt.int32
ALU = mybir.AluOpType
ACT = mybir.ActivationFunctionType
AX = mybir.AxisListType

B, C, H, W = 4, 64, 24, 24
HW = H * W
TAPS = 9
LAYERS = 2
PAIRS = B // 2
HALF = HW // 2
PADW = W + 2
BANK = 512

ROWS = 5
CHUNKS = -(-H // ROWS)
REACH = 2
BIG = 32.0
OFF = 27
NOFF = 2 * TAPS
LO = 32
KPOS = 67
KMASK = LO + OFF
YROWS = 2 * TAPS * ROWS
GN_EPS = 1e-5


def pixels(j):
    return W * (min(H, ROWS * (j + 1)) - ROWS * j)


def band(j, ky):
    a, b = ROWS * j, min(H, ROWS * (j + 1)) - 1
    return max(0, a - REACH - (ky - 1)), min(H, b + REACH - (ky - 1) + 1)


def wide(j):
    return min(band(j, ky)[0] for ky in range(3)), max(band(j, ky)[1] for ky in range(3))


WIDE_AT = [sum(wide(i)[1] - wide(i)[0] for i in range(j)) * W for j in range(CHUNKS + 1)]
WIDEST = max(wide(j)[1] - wide(j)[0] for j in range(CHUNKS)) * W
BANDEST = max(band(j, ky)[1] - band(j, ky)[0] for j in range(CHUNKS) for ky in range(3)) * W
assert 2 * BANDEST <= BANK and WIDEST <= BANK

STAGES = LAYERS * PAIRS
STEPS = [(k, j) for k in range(TAPS) for j in range(CHUNKS)]
NSTEPS = len(STEPS)
TX_SLOTS, S_SLOTS, JOB_BUFS, ITEM_BUFS = 7, 5, 2, 2
AHEAD = ITEM_BUFS
POOL_TAPS = (1, 3, 5, 7)




def before():
    parts = [("stats", 0, 0), ("stats", 0, 1), ("scaled", 0, 0), ("norm", 0, 0), ("normed", 0, 0), ("weights", 0, 0),
             ("split", 0, 0), ("pad", 0, 0), ("split", 0, 1), ("pad", 0, 1), ("conv", 0, 0), ("conv", 0, 1),
             ("conv", 0, 2), ("scaled", 0, 1), ("weights", 0, 1), ("z", 0, 0), ("offsets", 0, 0), ("z", 0, 1),
             ("off sum", 0, 0), ("high", 0, 0), ("off sum", 0, 1), ("high", 0, 1), ("z", 0, 2), ("low", 0, 0),
             ("low", 0, 1), ("z", 0, 3), ("y", 0, 0), ("z", 0, 4), ("y", 0, 1), ("y high", 0, 0), ("y end", 0, 0),
             ("z", 0, 5), ("largest", 0, 0), ("largest", 0, 1), ("tx", 0, (0, 0)), ("z", 0, 6), ("tx", 0, (0, 1)),
             ("z", 0, 7)]
    for j in range(2, CHUNKS):
        parts += [("y", 0, j), ("y high", 0, j - 1), ("y end", 0, j - 1)]
    return parts + [("z", 0, 8), ("z", 0, 9), ("y high", 0, CHUNKS - 1), ("y end", 0, CHUNKS - 1)]


def during(m):
    at = [[] for _ in STEPS]

    def put(part, n, where, args=None):
        for i, g in enumerate(where):
            at[g].append((part, n, args[i] if args else i))

    def tents(n, first, where):
        put("tx", n, where, [(first + i // 2, i % 2) for i in range(len(where))])

    if m == 0:
        tents(0, 1, (0, 1, 2, 3, 5, 6, 7, 8, 9, 10, 14, 15, 16, 17, 18, 19))
        put("flag", 0, (24,))
        put("scaled", 1, (29, 37))
        put("weights", 1, (44, 44))
    else:
        tents(m, 4, (0, 1, 2, 3, 5, 6, 7, 8, 9, 10))
    if m == STAGES - 1:
        put("final stats", m - 1, (3,))
        put("final mean", m - 1, (11,))
        put("final spread", m - 1, (11,))
        put("final variance", m - 1, (14,))
        put("final scale", m - 1, (14,))
        put("final out", m - 1, (17,))
        return at
    n = m + 1
    put("stats", n, (0, 2))
    put("norm", n, (4,))
    put("normed", n, (6,))
    put("split", n, (8, 9))
    put("pad", n, (9, 10))
    put("conv", n, (11, 12, 13))
    put("offsets", n, (13,))
    put("off sum", n, (15, 16))
    put("high", n, (17, 18))
    put("largest", n, (17, 18))
    put("low", n, (19, 20))
    if n >= PAIRS:
        put("sigmoid", n, (19,))
        put("mask high", n, (21, 22))
        put("mask low", n, (23, 24))
        put("y", n, (23, 27, 31, 34, 37))
        put("mask", n, (25, 28, 32, 35, 38))
        put("y high", n, (27, 30, 34, 37, 40))
        put("y end", n, (28, 31, 35, 38, 41))
        put("z", n, (14, 15, 16, 17, 18, 19, 20, 26, 33, 36))
        tents(n, 0, (21, 22, 29, 30, 39, 40, 42, 43))
    else:
        put("y", n, (23, 26, 30, 33, 36))
        put("y high", n, (23, 26, 30, 33, 36))
        put("y end", n, (25, 28, 32, 35, 38))
        put("z", n, (20, 25, 27, 31, 32, 34, 35, 37, 40, 41))
        tents(n, 0, (21, 22, 28, 29, 38, 39, 42, 43))
    put("flag", n, (24,))
    return at


NEXT = {(m, g): (m + g // NSTEPS, g % NSTEPS) for m in range(STAGES) for g in range(NSTEPS + AHEAD)
        if m + g // NSTEPS < STAGES}


def t_jobs():
    jobs, ends = {}, []

    def add(part, m, a):
        if part == "conv":
            names = [("conv", m, 0)] * (a == 0)
        elif part in ("weights", "norm", "z", "y", "mask", "tx", "flag", "final mean", "final variance"):
            names = [(part, m, a)]
        else:
            names = []
        for n in names:
            jobs[n] = len(jobs)

    for part in before():
        add(*part)
    for m in range(STAGES):
        for parts in during(m):
            for part in parts:
                add(*part)
        ends.append(len(jobs))
    for part in ("final mean", "final variance"):
        add(part, STAGES - 1, 0)
    return jobs, ends


JOB, JOBS_BY = t_jobs()


def constants():
    q_row, q_col = np.arange(ROWS * W) // W, np.arange(ROWS * W) % W
    ex = np.zeros((128, TAPS, ROWS * W), np.float16)
    ef = np.zeros((128, TAPS, ROWS * W), np.float16)
    em = np.zeros((128, TAPS, ROWS * W), np.float16)
    for k in range(TAPS):
        ex[[2 * k + 1, LO + 2 * k + 1, 65], k] = 1
        ex[66, k] = k % 3 - 1 - q_col
        ef[[2 * k, LO + 2 * k, 64], k] = 1
        ef[66, k] = k // 3 - 1 - q_row
        em[[NOFF + k, LO + NOFF + k], k] = 1
    ey = np.zeros((128, CHUNKS, 2, TAPS, ROWS), np.float16)
    my = np.zeros((128, 2, TAPS, ROWS), np.float16)
    sel = np.zeros((128, TAPS, ROWS * W), np.float16)
    for k in range(TAPS):
        ey[[2 * k, LO + 2 * k, 64], :, :, k] = 1
        for j in range(CHUNKS):
            ey[66, j, :, k] = k // 3 - 1 - (ROWS * j + np.arange(ROWS))
        my[[NOFF + k, LO + NOFF + k], :, k] = 1
        for part in range(2):
            for i in range(ROWS):
                sel[(part * TAPS + k) * ROWS + i, k, q_row == i] = 1
    half = np.concatenate([a.reshape(128, -1) for a in (ex, ey, my, sel, ef, em)], 1)
    at = np.arange(128)
    same = at[:, None] // 2 == at[None, :] // 2
    ident = np.eye(128, dtype=np.float32)
    pair = np.where(same, 0.5, 0).astype(np.float32)
    diff = np.where(same, -0.5, 0).astype(np.float32) + ident
    block = np.where(at[:, None] // C == at[None, :] // C, 1 / C, 0).astype(np.float32)
    low = np.stack([at >= C, at >= TAPS * ROWS], 1) * np.float32(-1)
    rows = np.tile(-ROWS * np.arange(CHUNKS, dtype=np.float32), (128, 1))
    full = np.concatenate([ident, pair, diff, block, low, rows], 1)
    p = np.arange(HW)
    pos = np.stack([p // W, p % W, np.ones(HW)]).astype(np.float16)
    return half, full, np.repeat(pos[:, None], B, 1)


NHALF = TAPS * ROWS * W
HALF_AT = np.cumsum([0, NHALF, CHUNKS * YROWS, YROWS, NHALF, NHALF, NHALF])


def build(nc, x, w_off, w_def, vecs, c_half, c_full, c_pos, out):
    ctx = ExitStack()
    with ctx:
        def sb(name, shape, dt=F32):
            return ctx.enter_context(nc.sbuf_tensor(name, shape, dt))

        def sem(name):
            return ctx.enter_context(nc.semaphore(name))

        x_l = sb("x_l", [128, B, HW])
        xn = sb("xn", [128, 2, HW])
        xh = sb("xh", [128, B, HW], F16)
        xpad = sb("xpad", [128, B, PADW * PADW], F16)
        xpad_v = xpad[:, :, :].rearrange("p b (h w) -> p b h w", h=PADW)
        w_raw = [[sb(f"w_raw{l}{i}", [128, TAPS * C]) for i in range(2)] for l in range(LAYERS)]
        w_unit = [sb(f"w_unit{i}", [128, TAPS, 2, C]) for i in range(2)]
        w_max = sb("w_max", [128, 2 * LAYERS])
        w_inv = sb("w_inv", [128, 2 * LAYERS])
        w_neg = sb("w_neg", [128, LAYERS])
        w_off16 = [sb(f"w_off16_{l}", [128, TAPS, 64], F16) for l in range(LAYERS)]
        w_hi = [sb(f"w_hi{l}", [128, TAPS * C], F16) for l in range(LAYERS)]
        w_lo = [sb(f"w_lo{l}", [128, TAPS * C], F16) for l in range(LAYERS)]
        vec = sb("vec", [128, 6])
        half = sb("half", [128, int(HALF_AT[-1])], F16)
        full = sb("full", [128, 4 * 128 + 2 + CHUNKS])
        bn = sb("bn", [128, STAGES, 2, 2, 6])
        chan = sb("chan", [128, STAGES, 2, 2])
        group = sb("group", [128, STAGES, 3, 2])
        gsq = sb("gsq", [128, STAGES, 2])
        gvar = sb("gvar", [128, STAGES, 2])
        rstd = sb("rstd", [128, STAGES, 2])
        minus_half = sb("minus_half", [128, 2])
        warm = sb("warm", [128, 2])
        off_a = sb("off_a", [OFF, 2, HW])
        off_b = sb("off_b", [OFF, 2, HW])
        pos = sb("pos", [128, B, HW], F16)
        msk = sb("msk", [KMASK, B, HW], F16)
        omax = sb("omax", [OFF, STAGES, 2])
        omax1 = sb("omax1", [OFF, STAGES])
        oall = sb("oall", [1, STAGES])
        flag = sb("flag", [1, STAGES], I32)
        ya = sb("ya", [YROWS, 2, 2, WIDEST])
        yt = sb("yt", [YROWS, 2, 2, WIDEST])
        ym = sb("ym", [YROWS, 2, 2, WIDEST])
        yh = sb("yh", [YROWS, 2, 2, WIDEST], F16)
        ytent = sb("ytent", [YROWS, B, WIDE_AT[-1]], F16)
        z = sb("z", [ROWS * W, B, CHUNKS, TAPS * C])
        tx = sb("tx", [ROWS * W, TX_SLOTS, 2, HW])
        s = sb("s", [ROWS * W, S_SLOTS, 2, BANDEST])
        zeros = sb("zeros", [1, HALF], F16)
        y = sb("y", [128, PAIRS, HW])
        fin = sb("fin", [128, PAIRS, 8])
        res = sb("res", [128, PAIRS, HW])
        s_all = sb("scratch", [ROWS * W, 3 * HW + CHUNKS * C + 3 * (ROWS * W // 2) + HW // 2])
        at = [0]

        def place(n, rows=ROWS * W):
            at[0] += n
            return s_all[0:rows, at[0] - n:at[0]]
        g_xt, g_yt, g_s, g_z = place(HW), place(HW), place(HW), place(CHUNKS * C)
        g_ex, g_ef, g_em = (place(ROWS * W // 2, n).bitcast(F16) for n in (KPOS, KPOS, KMASK))
        g_pos = place(HW // 2, KPOS).bitcast(F16)
        g_msk = sb("g_msk", [KMASK, HW], F16)[:, :]

        def h(i, shape):
            v = half[:, int(HALF_AT[i]):int(HALF_AT[i + 1])]
            return v.rearrange("p (a b) -> p a b", a=shape)
        ex, ey, my, sel, ef, em = h(0, TAPS), h(1, CHUNKS), h(2, 1), h(3, TAPS), h(4, TAPS), h(5, TAPS)
        ident, pair_m, diff_m, block_m = (full[:, 128 * i:128 * (i + 1)] for i in range(4))
        low_c, low_y = full[:, 512:513], full[0:YROWS, 513:514]

        tb = ctx.enter_context(nc.psum_tensor("tb", [128, JOB_BUFS, 2 * BANK], F32))
        ib = ctx.enter_context(nc.psum_tensor("ib", [128, ITEM_BUFS, BANK], F32))
        acc = ctx.enter_context(nc.psum_tensor("acc", [128, 2, BANK], F32))

        x_here = [sem(f"x_here{b}") for b in range(B)]
        w_here = [[sem(f"w_here{l}{i}") for i in range(2)] for l in range(LAYERS)]
        warmed = sem("warmed")
        vec_here, half_here, full_here = sem("vec_here"), sem("half_here"), sem("full_here")
        pos_here = sem("pos_here")
        cleared = sem("cleared")
        t_full = [sem(f"t_full{i}") for i in range(JOB_BUFS)]
        t_free = [sem(f"t_free{i}") for i in range(JOB_BUFS)]
        item_full = [sem(f"item_full{i}") for i in range(ITEM_BUFS)]
        acc_full, acc_free = sem("acc_full"), sem("acc_free")
        dve_c = sem("dve_c")
        w_scaled = sem("w_scaled")
        wt_high, wt_done = sem("wt_high"), sem("wt_done")
        x_mid = sem("x_mid")
        stats_ready, gvar_ready, rstd_ready = sem("stats_ready"), sem("gvar_ready"), sem("rstd_ready")
        xn_ready, xh_ready, x16_ready = sem("xn_ready"), sem("xh_ready"), sem("x16_ready")
        xpad_ready = sem("xpad_ready")
        off_parts = sem("off_parts")
        off_sum, omax_ready, flag_ready = sem("off_sum"), sem("omax_ready"), sem("flag_ready")
        pos_high, pos_ready = sem("pos_high"), sem("pos_ready")
        sig_ready, msk_high, msk_ready = sem("sig_ready"), sem("msk_high"), sem("msk_ready")
        ya_ready, yt_ready, ym_ready, yh_ready = sem("ya_ready"), sem("yt_ready"), sem("ym_ready"), sem("yh_ready")
        ytent_ready = sem("ytent_ready")
        z_ready = [sem(f"z_ready{bb}") for bb in range(2)]
        tx_abs, tx_act, tx_pool = sem("tx_abs"), sem("tx_act"), sem("tx_pool")
        s_ready, s_used = sem("s_ready"), sem("s_used")
        y_ready = sem("y_ready")
        fin_stats, fin_var, fin_rstd, fin_ready = sem("fin_stats"), sem("fin_var"), sem("fin_rstd"), sem("fin_ready")
        relu_ready, res_ready, stored = sem("relu_ready"), sem("res_ready"), sem("stored")
        g_act, g_dve, g_pe, g_sum, g_out = ([sem(f"{n}{m}") for m in range(STAGES)]
                                            for n in ("g_act", "g_dve", "g_pe", "g_sum", "g_out"))

        block = ctx.enter_context(nc.Block())

        def tbuf(name):
            return tb[:, JOB[name] % JOB_BUFS, :]

        def wait_full(eng, name):
            n = JOB[name]
            eng.wait_ge(t_full[n % JOB_BUFS], n // JOB_BUFS + 1)

        def free_of(name):
            return t_free[JOB[name] % JOB_BUFS]

        def halves(v):
            return v.rearrange("p (h c) -> p h c", h=2)

        def banks(v):
            return halves(v)[:, :, 0:HALF]

        def where(m):
            return m // PAIRS, m % PAIRS

        def tents_wait(eng, m, k):
            pool = [i in POOL_TAPS for i in range(TAPS)] * m + [i in POOL_TAPS for i in range(k + 1)]
            if k in POOL_TAPS:
                eng.wait_ge(tx_pool, 2 * sum(pool))
            else:
                eng.wait_ge(tx_act, 2 * (len(pool) - sum(pool)))

        def g_steps(l):
            return 7 + 2 * l + CHUNKS, CHUNKS * (2 + l), 1 + 2 * CHUNKS

        def far(eng, m):
            eng.wait_ge(flag_ready, m + 1)
            return eng.value_load(flag[0:1, m:m + 1], min_val=0, max_val=1) != 0

        @block.sync
        def _(sp):
            for b in range(B):
                for d in range(2):
                    sp.dma_start(x_l[64 * d:64 * d + 64, b, :], x[b]).then_inc(x_here[b], 16)
                if b == 1:
                    sp.dma_start(full[:, :], c_full).then_inc(full_here, 16)
                    sp.wait_ge(cleared, 2)
                    sp.dma_start(pos[64:KPOS, :, :], c_pos).then_inc(pos_here, 16)
            sp.dma_start(w_raw[1][0][:, :], w_off[1]).then_inc(w_here[1][0], 16)
            sp.dma_start(w_raw[1][1][:, :], w_def[1]).then_inc(w_here[1][1], 16)
            for p in range(PAIRS):
                sp.wait_ge(res_ready, 2 * p + 2)
                for bb in range(2):
                    sp.dma_start(out[2 * p + bb], res[64 * bb:64 * bb + 64, p, :]).then_inc(stored, 16)
            sp.wait_ge(stored, 16 * B)

        @block.gpsimd
        def _(pool):
            nc.gpsimd.memset(minus_half[:, :], -0.5).then_inc(cleared, 1)
            nc.gpsimd.memset(pos[:, :, :].bitcast(F32), 0.0).then_inc(cleared, 1)
            nc.gpsimd.memset(xpad[:, :, :].bitcast(F32), 0.0).then_inc(cleared, 1)
            nc.gpsimd.memset(zeros[:, :], 0.0).then_inc(cleared, 1)
            nc.gpsimd.memset(msk[:, :, :].bitcast(F32), 0.0).then_inc(cleared, 1)

            def norm(m, _):
                pool.wait_ge(gvar_ready, m + 1)
                nc.gpsimd.tensor_tensor(rstd[:, m, :], gvar[:, m, :], minus_half[:, :], ALU.pow).then_inc(rstd_ready, 1)

            def column_tents(m, a):
                k, bb = a
                if k not in POOL_TAPS:
                    return
                pool.wait_ge(tx_abs, 2 * (TAPS * m + k) + bb + 1)
                v = tx[:, (TAPS * m + k) % TX_SLOTS, bb, :]
                nc.gpsimd.tensor_scalar(v, v, 1.0, 0.0, ALU.min, ALU.max).then_inc(tx_pool, 1)

            def final_scale(m, _):
                l, p = where(m)
                pool.wait_ge(fin_var, p + 1)
                nc.gpsimd.tensor_tensor(fin[:, p, 5:6], fin[:, p, 4:5], minus_half[:, 0:1], ALU.pow).then_inc(fin_rstd, 1)

            part = {"norm": norm, "tx": column_tents, "final scale": final_scale}
            pool.wait_ge(cleared, 1)
            for name, m, a in before():
                if name in part:
                    part[name](m, a)
            for stage in range(STAGES):
                for at in during(stage):
                    for name, m, a in at:
                        if name in part:
                            part[name](m, a)
            final_scale(STAGES - 1, 0)

        @block.scalar
        def _(act):
            act.dma_start(w_raw[0][0][:, :], w_off[0]).then_inc(w_here[0][0], 16)
            act.dma_start(vec[:, :], vecs).then_inc(vec_here, 16)
            act.dma_start(w_raw[0][1][:, :], w_def[0]).then_inc(w_here[0][1], 16)
            act.dma_start(half[:, :], c_half).then_inc(half_here, 16)
            act.wait_ge(cleared, 1)
            nc.scalar.activation(warm[:, :], minus_half[:, :], ACT.Sigmoid).then_inc(warmed, 1)
            act.wait_ge(vec_here, 16)

            def weights(l, i):
                name = ("weights", l, i)
                wait_full(act, name)
                if i:
                    dst, src = w_hi[l][:, :], tbuf(name)[:, 0:TAPS * C]
                else:
                    dst = w_off16[l][:, :, 0:32]
                    src = tbuf(name)[:, 0:TAPS * 64].rearrange("p (t o) -> p t o", t=TAPS)[:, :, 0:32]
                nc.scalar.activation(dst, src, ACT.Copy).then_inc(wt_high, 1)

            def normed(m, _):
                l, p = where(m)
                if m >= PAIRS:
                    for bb in range(2):
                        act.wait_ge(z_ready[bb], CHUNKS * (m - 1))
                    act.wait_ge(xpad_ready, 2 * (m - 1))
                for bb in range(2):
                    act.wait_ge(xn_ready, 2 * m + bb + 1)
                    nc.scalar.activation(xh[:, 2 * p + bb, :], xn[:, bb, :], ACT.Copy).then_inc(xh_ready, 1)

            def offsets(m, _):
                l, p = where(m)
                wait_full(act, ("conv", m, 0))
                v = banks(tbuf(("conv", m, 0)))
                if m:
                    act.wait_ge(pos_ready, 2 * m)
                    act.wait_ge(omax_ready, 3 * m)
                if m > PAIRS:
                    act.wait_ge(msk_ready, 2 * (m - PAIRS))
                for bb in range(2):
                    for i, dst in enumerate((off_a, off_b)):
                        r = slice(64 * bb + LO * i, 64 * bb + LO * i + OFF)
                        nc.scalar.activation(halves(dst[:, bb, :]), v[r], ACT.Identity, scale=w_max[r, 2 * l:2 * l + 1],
                                             bias=vec[r, l:l + 1] if i == 0 else 0.0).then_inc(off_parts, 1)
                act.wait_ge(off_parts, 4 * m + 4)
                act.sem_inc(free_of(("conv", m, 0)), 1)

            def high(m, bb):
                l, p = where(m)
                if m >= PAIRS:
                    act.wait_ge(tx_abs, 2 * TAPS * (m - 1))
                act.wait_ge(off_sum, 2 * m + bb + 1)
                act.wait_ge(cleared, 2)
                nc.scalar.activation(pos[0:OFF, 2 * p + bb, :], off_b[:, bb, :], ACT.Copy).then_inc(pos_high, 1)

            def sigmoid(m, _):
                act.wait_ge(omax_ready, 3 * m + 2)
                for bb in range(2):
                    nc.scalar.activation(off_a[:, bb, :], off_a[:, bb, :], ACT.Sigmoid).then_inc(sig_ready, 1)

            def mask_high(m, bb):
                l, p = where(m)
                act.wait_ge(cleared, 5)
                act.wait_ge(sig_ready, 2 * (m - PAIRS) + bb + 1)
                nc.scalar.activation(msk[0:OFF, 2 * p + bb, :], off_a[:, bb, :], ACT.Copy).then_inc(msk_high, 1)

            def z_out(m, i):
                l, p = where(m)
                j, bb = divmod(i, 2)
                if m == 0 and bb == 0:
                    return
                q = pixels(j)
                wait_full(act, ("z", m, i))
                if m >= PAIRS:
                    act.wait_ge(s_used, NSTEPS * (m - 1))
                nc.scalar.activation(halves(z[0:q, 2 * p + bb, j, :]), banks(tbuf(("z", m, i))[0:q]), ACT.Copy)\
                    .then_inc(z_ready[bb], 1)
                act.wait_ge(z_ready[bb], CHUNKS * m + j + 1)
                act.sem_inc(free_of(("z", m, i)), 1)

            def y_tents(m, j):
                n = CHUNKS * m + j
                nw = (wide(j)[1] - wide(j)[0]) * W
                wait_full(act, ("y", m, j))
                if n >= 2:
                    act.wait_ge(yt_ready, n - 1)
                nc.scalar.activation(ya[:, n % 2, :, 0:nw], halves(tbuf(("y", m, j))[0:YROWS])[:, :, 0:nw], ACT.Abs)\
                    .then_inc(ya_ready, 1)
                act.wait_ge(ya_ready, n + 1)
                act.sem_inc(free_of(("y", m, j)), 1)
                if n >= 2:
                    act.wait_ge(ytent_ready, n - 1)
                nc.scalar.activation(yt[:, n % 2, :, 0:nw], ya[:, n % 2, :, 0:nw], ACT.Relu, scale=-1.0, bias=1.0)\
                    .then_inc(yt_ready, 1)

            def y_high(m, j):
                l, p = where(m)
                n = CHUNKS * m + j
                nw = (wide(j)[1] - wide(j)[0]) * W
                if l:
                    act.wait_ge(ym_ready, n - CHUNKS * PAIRS + 1)
                else:
                    act.wait_ge(yt_ready, n + 1)
                nc.scalar.activation(yh[:, n % 2, :, 0:nw], (ym if l else yt)[:, n % 2, :, 0:nw], ACT.Copy)\
                    .then_inc(yh_ready, 1)

            def column_tents(m, a):
                k, bb = a
                tap = TAPS * m + k
                if tap >= TX_SLOTS:
                    act.wait_ge(s_ready, CHUNKS * (tap - TX_SLOTS + 1))
                wait_full(act, ("tx", m, a))
                v = tx[:, tap % TX_SLOTS, bb, :]
                nc.scalar.activation(halves(v), banks(tbuf(("tx", m, a))[0:ROWS * W]), ACT.Abs).then_inc(tx_abs, 1)
                act.wait_ge(tx_abs, 2 * tap + bb + 1)
                act.sem_inc(free_of(("tx", m, a)), 1)
                if k not in POOL_TAPS:
                    nc.scalar.activation(v, v, ACT.Relu, scale=-1.0, bias=1.0).then_inc(tx_act, 1)

            def sums_out(m):
                l, p = where(m)
                act.wait_ge(acc_full, m + 1)
                if m >= PAIRS:
                    act.wait_ge(x_mid, 4 * (p + 1))
                nc.scalar.activation(halves(y[:, p, :]), acc[:, :, 0:HALF], ACT.Identity,
                                     scale=w_neg[:, l:l + 1], bias=vec[:, 2 + l:3 + l]).then_inc(y_ready, 1)
                act.wait_ge(y_ready, m + 1)
                act.sem_inc(acc_free, 1)

            def general(m):
                l, p = where(m)
                na, nd, np_ = g_steps(l)
                with act.Fori(0, TAPS) as k:
                    for bb in range(2):
                        it = 2 * k + bb
                        b = 2 * p + bb
                        act.wait_ge(g_pe[m], np_ * it + 1)
                        nc.scalar.activation(g_pos, pos[0:KPOS, b, :], ACT.Copy).then_inc(g_act[m], 1)
                        nc.scalar.activation(g_ex, ex[0:KPOS, bass.ds(k, 1), :], ACT.Copy).then_inc(g_act[m], 1)
                        nc.scalar.activation(g_ef, ef[0:KPOS, bass.ds(k, 1), :], ACT.Copy).then_inc(g_act[m], 1)
                        zf = z[:, b, :, :].rearrange("q j (k o) -> q j k o", k=TAPS)
                        nc.scalar.activation(g_z[:, 0:4 * C].rearrange("q (j o) -> q j o", j=4),
                                             zf[:, 0:4, bass.ds(k, 1), :], ACT.Copy).then_inc(g_act[m], 1)
                        nc.scalar.activation(g_z[0:pixels(4), 4 * C:5 * C], zf[0:pixels(4), 4, bass.ds(k, 1), :],
                                             ACT.Copy).then_inc(g_act[m], 1)
                        if l:
                            nc.scalar.activation(g_msk, msk[:, b, :], ACT.Copy).then_inc(g_act[m], 1)
                            nc.scalar.activation(g_em, em[0:KMASK, bass.ds(k, 1), :], ACT.Copy).then_inc(g_act[m], 1)
                        act.wait_ge(g_pe[m], np_ * it + 2)
                        nc.scalar.activation(halves(g_xt), banks(tb[0:ROWS * W, 0, :]), ACT.Abs).then_inc(g_act[m], 1)
                        act.wait_ge(g_act[m], na * it + 6 + 2 * l)
                        nc.scalar.activation(g_xt, g_xt, ACT.Relu, scale=-1.0, bias=1.0).then_inc(g_act[m], 1)
                        for j in range(CHUNKS):
                            act.wait_ge(g_pe[m], np_ * it + 3 + 2 * j)
                            nc.scalar.activation(halves(g_yt), banks(tb[0:ROWS * W, 1, :]), ACT.Abs,
                                                 bias=full[0:ROWS * W, 514 + j:515 + j]).then_inc(g_act[m], 1)
                act.wait_ge(g_sum[m], 1)
                nc.scalar.activation(halves(y[:, p, :]), acc[:, :, 0:HALF], ACT.Identity,
                                     scale=w_neg[:, l:l + 1], bias=vec[:, 2 + l:3 + l]).then_inc(g_out[m], 1)
                act.wait_ge(g_out[m], 1)

            def final_out(m, _):
                l, p = where(m)
                act.wait_ge(fin_ready, p + 1)
                nc.scalar.activation(res[:, p, :], y[:, p, :], ACT.Relu, scale=fin[:, p, 6:7], bias=fin[:, p, 7:8])\
                    .then_inc(relu_ready, 1)

            part = {"weights": weights, "normed": normed, "offsets": offsets, "high": high,
                    "sigmoid": sigmoid, "mask high": mask_high, "z": z_out, "y": y_tents, "y high": y_high, "tx": column_tents, "final out": final_out}
            for name, n, a in before():
                if name in part:
                    part[name](n, a)
            for m in range(STAGES):
                for at in during(m):
                    for name, n, a in at:
                        if name in part:
                            part[name](n, a)
                sums_out(m)
                with act.If(far(act, m)):
                    general(m)
            final_out(STAGES - 1, 0)

        @block.vector
        def _(dve):
            count = [0]

            def then(ins):
                count[0] += 1
                ins.then_inc(dve_c, 1)
                dve.wait_ge(dve_c, count[0])

            def scaled(l, i):
                m = slice(2 * l + i, 2 * l + i + 1)
                dve.wait_ge(w_here[l][i], 16)
                then(nc.vector.tensor_reduce(w_max[:, m], w_raw[l][i][:, :], axis=AX.X, op=ALU.max,
                                             apply_absolute_value=True))
                then(nc.vector.tensor_scalar(w_max[:, m], w_max[:, m], 1e-30, None, ALU.max))
                then(nc.vector.reciprocal(w_inv[:, m], w_max[:, m]))
                if l:
                    dve.wait_ge(wt_high, 2 * l)
                for d in range(2):
                    nc.vector.tensor_scalar(w_unit[i][:, :, d, :],
                                            w_raw[l][i][:, :].rearrange("o (t c) -> o t c", t=TAPS),
                                            w_inv[:, m], None, ALU.mult).then_inc(w_scaled, 1)
                if i:
                    then(nc.vector.tensor_scalar(w_neg[:, l:l + 1], w_max[:, m], -1.0, None, ALU.mult))

            def weights(l, i):
                name = ("weights", l, i)
                dve.wait_ge(wt_high, 2 * l + i + 1)
                if i:
                    dst, src, high = w_lo[l][:, :], tbuf(name)[:, 0:TAPS * C], w_hi[l][:, :]
                else:
                    dst, high = w_off16[l][:, :, 32:64], w_off16[l][:, :, 0:32]
                    src = tbuf(name)[:, 0:TAPS * 64].rearrange("p (t o) -> p t o", t=TAPS)[:, :, 32:64]
                nc.vector.tensor_tensor(dst, src, high, ALU.subtract).then_inc(wt_done, 1)
                dve.wait_ge(wt_done, 2 * l + i + 1)
                dve.sem_inc(free_of(name), 1)

            def stats(m, bb):
                l, p = where(m)
                r = slice(64 * bb, 64 * bb + 64)
                if l:
                    dve.wait_ge(y_ready, p + 1)
                    for d in (1 - bb, bb):
                        nc.vector.tensor_tensor(x_l[64 * d:64 * d + 64, 2 * p + bb, :], y[r, p, :],
                                                x_l[r, 2 * p + bb, :], ALU.add).then_inc(x_mid, 1)
                    dve.wait_ge(x_mid, 4 * p + 2 * bb + 2)
                dve.wait_ge(x_here[2 * p + bb], 32)
                for i in range(2):
                    nc.vector.bn_stats(bn[:, m, bb, i, :], x_l[:, 2 * p + bb, HALF * i:HALF * (i + 1)]).then_inc(dve_c, 1)
                count[0] += 2
                dve.wait_ge(dve_c, count[0])
                nc.vector.bn_aggr(chan[:, m, :, bb], bn[:, m, bb, :, :]).then_inc(stats_ready, 1)

            def norm(m, _):
                l, p = where(m)
                wait_full(dve, ("norm", m, 0))
                then(nc.vector.tensor_copy(group[:, m, :, :],
                                           tbuf(("norm", m, 0))[:, 0:6].rearrange("p (a b) -> p a b", a=3)))
                dve.sem_inc(free_of(("norm", m, 0)), 1)
                then(nc.vector.tensor_tensor(gsq[:, m, :], group[:, m, 2, :], group[:, m, 2, :], ALU.mult))
                then(nc.vector.tensor_tensor(gsq[:, m, :], gsq[:, m, :], group[:, m, 1, :], ALU.add))
                nc.vector.tensor_scalar(gvar[:, m, :], gsq[:, m, :], GN_EPS, None, ALU.add).then_inc(gvar_ready, 1)

            def normed(m, _):
                l, p = where(m)
                dve.wait_ge(rstd_ready, m + 1)
                if m:
                    dve.wait_ge(xh_ready, 2 * m)
                    dve.wait_ge(x16_ready, 2 * m)
                for bb in range(2):
                    nc.vector.tensor_scalar(xn[:, bb, :], x_l[:, 2 * p + bb, :], group[:, m, 0, bb:bb + 1],
                                            rstd[:, m, bb:bb + 1], ALU.subtract, ALU.mult).then_inc(xn_ready, 1)

            def split(m, bb):
                l, p = where(m)
                dve.wait_ge(xn_ready, 2 * m + bb + 1)
                dve.wait_ge(xh_ready, 2 * m + bb + 1)
                nc.vector.scalar_tensor_tensor(out=xh[:, 2 * p + bb, :], in0=xh[:, 2 * p + bb, :], scalar=low_c,
                                               in1=xn[:, bb, :], op0=ALU.mult, op1=ALU.add).then_inc(x16_ready, 1)

            def pad(m, bb):
                b = 2 * where(m)[1] + bb
                if m >= PAIRS:
                    dve.wait_ge(off_parts, 4 * (m - 1))
                dve.wait_ge(cleared, 3)
                dve.wait_ge(x16_ready, 2 * m + bb + 1)
                nc.vector.tensor_copy(xpad_v[:, b, 1:H + 1, 1:W + 1], xh[:, b, :].rearrange("p (h w) -> p h w", h=H))\
                    .then_inc(xpad_ready, 1)

            def off_sums(m, bb):
                dve.wait_ge(off_parts, 4 * m + 2 * bb + 2)
                then(nc.vector.tensor_tensor(off_a[:, bb, :], off_a[:, bb, :], off_b[:, bb, :], ALU.add))
                nc.vector.tensor_scalar(off_b[:, bb, :], off_a[:, bb, :], -BIG, BIG, ALU.max, ALU.min)\
                    .then_inc(off_sum, 1)

            def largest(m, bb):
                nc.vector.tensor_reduce(omax[0:NOFF, m, bb:bb + 1], off_a[0:NOFF, bb, :], axis=AX.X, op=ALU.max,
                                        apply_absolute_value=True).then_inc(omax_ready, 1)
                if bb:
                    dve.wait_ge(omax_ready, 3 * m + 2)
                    nc.vector.tensor_reduce(omax1[0:NOFF, m:m + 1], omax[0:NOFF, m, :], axis=AX.X, op=ALU.max)\
                        .then_inc(omax_ready, 1)

            def low(m, bb):
                b = 2 * where(m)[1] + bb
                dve.wait_ge(pos_high, 2 * m + bb + 1)
                nc.vector.tensor_tensor(pos[LO:LO + OFF, b, :], off_b[:, bb, :], pos[0:OFF, b, :], ALU.subtract)\
                    .then_inc(pos_ready, 1)

            def mask_low(m, bb):
                b = 2 * where(m)[1] + bb
                dve.wait_ge(msk_high, 2 * (m - PAIRS) + bb + 1)
                nc.vector.tensor_tensor(msk[LO:LO + OFF, b, :], off_a[:, bb, :], msk[0:OFF, b, :], ALU.subtract)\
                    .then_inc(msk_ready, 1)

            def find_far(m, _):
                wait_full(dve, ("flag", m, 0))
                then(nc.vector.tensor_reduce(oall[:, m:m + 1], tbuf(("flag", m, 0))[0:1, 0:NOFF], axis=AX.X, op=ALU.max))
                dve.sem_inc(free_of(("flag", m, 0)), 1)
                nc.vector.tensor_scalar(flag[:, m:m + 1], oall[:, m:m + 1], float(REACH), None, ALU.is_gt)\
                    .then_inc(flag_ready, 1)

            def masked(m, j):
                n = CHUNKS * m + j
                nw = (wide(j)[1] - wide(j)[0]) * W
                wait_full(dve, ("mask", m, j))
                dve.wait_ge(yt_ready, n + 1)
                nc.vector.tensor_tensor(ym[:, n % 2, :, 0:nw], halves(tbuf(("mask", m, j))[0:YROWS])[:, :, 0:nw],
                                        yt[:, n % 2, :, 0:nw], ALU.mult).then_inc(ym_ready, 1)
                dve.wait_ge(ym_ready, n - CHUNKS * PAIRS + 1)
                dve.sem_inc(free_of(("mask", m, j)), 1)

            def y_end(m, j):
                l, p = where(m)
                n = CHUNKS * m + j
                nw = (wide(j)[1] - wide(j)[0]) * W
                dve.wait_ge(yh_ready, n + 1)
                nc.vector.scalar_tensor_tensor(
                    out=ytent[:, 2 * p:2 * p + 2, WIDE_AT[j]:WIDE_AT[j] + nw], in0=yh[:, n % 2, :, 0:nw],
                    scalar=low_y, in1=(ym if l else yt)[:, n % 2, :, 0:nw], op0=ALU.mult, op1=ALU.add)\
                    .then_inc(ytent_ready, 1)

            def z_out(m, i):
                j, bb = divmod(i, 2)
                if m or bb:
                    return
                q = pixels(j)
                wait_full(dve, ("z", m, i))
                nc.vector.tensor_copy(halves(z[0:q, bb, j, :]), banks(tbuf(("z", m, i))[0:q])).then_inc(z_ready[0], 1)
                dve.wait_ge(z_ready[0], j + 1)
                dve.sem_inc(free_of(("z", m, i)), 1)

            def sampling(m, g):
                k, j = STEPS[g]
                q = pixels(j)
                r0, r1 = band(j, k // 3)
                nb = (r1 - r0) * W
                n = NSTEPS * m + g
                tents_wait(dve, m, k)
                if n >= S_SLOTS:
                    dve.wait_ge(s_used, n - S_SLOTS + 1)
                dve.wait_ge(item_full[n % ITEM_BUFS], n // ITEM_BUFS + 1)
                by_pool = k in POOL_TAPS
                nc.vector.scalar_tensor_tensor(
                    out=s[0:q, n % S_SLOTS, :, 0:nb],
                    in0=tx[0:q, (TAPS * m + k) % TX_SLOTS, :, W * r0:W * r1], scalar=1.0 if by_pool else -1.0,
                    in1=ib[0:q, n % ITEM_BUFS, 0:2 * nb].rearrange("p (b c) -> p b c", b=2),
                    op0=ALU.subtract if by_pool else ALU.mult, op1=ALU.mult).then_inc(s_ready, 1)

            def general(m):
                l, p = where(m)
                na, nd, np_ = g_steps(l)
                dve.wait_ge(y_ready, m + 1)
                dve.sem_inc(g_dve[m], 1)
                with dve.Fori(0, TAPS) as k:
                    for bb in range(2):
                        it = 2 * k + bb
                        for j in range(CHUNKS):
                            done = nd * it + (2 + l) * j + 1
                            dve.wait_ge(g_act[m], na * it + 8 + 2 * l + j)
                            nc.vector.tensor_scalar(g_yt, g_yt, 1.0, 1.0, ALU.min, ALU.subtract).then_inc(g_dve[m], 1)
                            dve.wait_ge(g_dve[m], done + 1)
                            nc.vector.tensor_tensor(g_s, g_yt, g_xt, ALU.mult).then_inc(g_dve[m], 1)
                            if l:
                                dve.wait_ge(g_dve[m], done + 2)
                                nc.vector.tensor_tensor(halves(g_s), ib[0:ROWS * W, :, 0:HALF], halves(g_s),
                                                        ALU.mult).then_inc(g_dve[m], 1)
                dve.wait_ge(g_out[m], 1)

            def final_stats(m, _):
                l, p = where(m)
                dve.wait_ge(y_ready, m + 1)
                for i in range(2):
                    nc.vector.bn_stats(bn[:, p, 0, i, :], y[:, p, HALF * i:HALF * (i + 1)]).then_inc(dve_c, 1)
                count[0] += 2
                dve.wait_ge(dve_c, count[0])
                nc.vector.bn_aggr(fin[:, p, 0:2], bn[:, p, 0, :, :]).then_inc(fin_stats, 1)

            def final_spread(m, _):
                l, p = where(m)
                name = ("final mean", m, 0)
                wait_full(dve, name)
                then(nc.vector.tensor_copy(fin[:, p, 2:4], tbuf(name)[:, 0:2]))
                dve.sem_inc(free_of(name), 1)
                then(nc.vector.tensor_tensor(fin[:, p, 4:5], fin[:, p, 0:1], fin[:, p, 2:3], ALU.subtract))
                nc.vector.tensor_tensor(fin[:, p, 5:6], fin[:, p, 4:5], fin[:, p, 4:5], ALU.mult).then_inc(fin_stats, 1)

            def final_scale(m, _):
                l, p = where(m)
                name = ("final variance", m, 0)
                wait_full(dve, name)
                then(nc.vector.tensor_tensor(fin[:, p, 3:4], tbuf(name)[:, 0:1], fin[:, p, 3:4], ALU.add))
                dve.sem_inc(free_of(name), 1)
                nc.vector.tensor_scalar(fin[:, p, 4:5], fin[:, p, 3:4], GN_EPS, None, ALU.add).then_inc(fin_var, 1)
                dve.wait_ge(fin_rstd, p + 1)
                then(nc.vector.tensor_scalar(fin[:, p, 6:7], fin[:, p, 5:6], vec[:, 4:5], None, ALU.mult))
                then(nc.vector.tensor_tensor(fin[:, p, 4:5], fin[:, p, 2:3], fin[:, p, 6:7], ALU.mult))
                nc.vector.tensor_scalar(fin[:, p, 7:8], fin[:, p, 4:5], -1.0, vec[:, 5:6], ALU.mult, ALU.add)\
                    .then_inc(fin_ready, 1)

            def final_out(m, _):
                l, p = where(m)
                dve.wait_ge(relu_ready, p + 1)
                for bb in range(2):
                    r = slice(64 * bb, 64 * bb + 64)
                    nc.vector.tensor_tensor(res[r, p, :], res[r, p, :], x_l[r, 2 * p + bb, :], ALU.add).then_inc(res_ready, 1)

            part = {"scaled": scaled, "weights": weights, "stats": stats, "norm": norm, "normed": normed,
                    "split": split, "pad": pad, "off sum": off_sums,
                    "largest": largest, "low": low, "mask low": mask_low,
                    "flag": find_far, "z": z_out, "mask": masked, "y end": y_end, "final stats": final_stats,
                    "final spread": final_spread, "final scale": final_scale, "final out": final_out}
            dve.wait_ge(full_here, 16)
            dve.wait_ge(vec_here, 16)
            for name, n, a in before():
                if name in part:
                    part[name](n, a)
            for g in range(AHEAD):
                sampling(0, g)
            for m in range(STAGES):
                for g, at in enumerate(during(m)):
                    if (m, g + AHEAD) in NEXT:
                        sampling(*NEXT[m, g + AHEAD])
                    for name, n, a in at:
                        if name in part:
                            part[name](n, a)
                with dve.If(far(dve, m)):
                    general(m)
            final_stats(STAGES - 1, 0)
            final_spread(STAGES - 1, 0)
            final_scale(STAGES - 1, 0)
            final_out(STAGES - 1, 0)

        @block.tensor
        def _(pe):
            mm = nc.tensor.matmul

            def take(name):
                n = JOB[name]
                if n >= JOB_BUFS:
                    pe.wait_ge(t_free[n % JOB_BUFS], n // JOB_BUFS)
                return t_full[n % JOB_BUFS]

            def weights(l, i):
                name = ("weights", l, i)
                pe.wait_ge(w_scaled, 4 * l + 2 * i + 2)
                full_sem = take(name)
                for t in range(TAPS):
                    last = nc.tensor.transpose(tbuf(name)[:, 64 * t:64 * t + 64], w_unit[i][0:64, t, :, :],
                                               ident[0:64, 0:64])
                last.then_inc(full_sem, 1)

            def norm(m, _):
                name = ("norm", m, 0)
                pe.wait_ge(stats_ready, 2 * (m + 1))
                full_sem = take(name)
                mm(tbuf(name)[:, 0:4], pair_m, chan[:, m, :, :], start=True, stop=True)
                mm(tbuf(name)[:, 4:6], diff_m, chan[:, m, 0, :], start=True, stop=True).then_inc(full_sem, 1)

            def conv(m, i):
                l, p = where(m)
                name = ("conv", m, 0)
                if i == 0:
                    pe.wait_ge(wt_done, 2 * l + 1)
                    pe.wait_ge(xpad_ready, 2 * (m + 1))
                    take(name)
                for t in range(3 * i, 3 * i + 3):
                    for hf in range(2):
                        for bb in range(2):
                            last = mm(tbuf(name)[64 * bb:64 * bb + 64, BANK * hf:BANK * hf + HALF], w_off16[l][:, t, :],
                                      xpad_v[:, 2 * p + bb, 12 * hf + i:12 * hf + i + 12, t % 3:t % 3 + W],
                                      start=t == 0, stop=t == TAPS - 1)
                if i == 2:
                    last.then_inc(t_full[JOB[name] % JOB_BUFS], 1)

            def z_products(m, i):
                l, p = where(m)
                j, bb = divmod(i, 2)
                q = pixels(j)
                name = ("z", m, i)
                pe.wait_ge(wt_done, 2 * l + 2)
                pe.wait_ge(x16_ready, 2 * m + bb + 1)
                full_sem = take(name)
                for hf in range(2):
                    for i_part, wp in enumerate((w_hi[l], w_lo[l])):
                        last = mm(tbuf(name)[0:q, BANK * hf:BANK * hf + HALF],
                                  xh[:, 2 * p + bb, ROWS * W * j:ROWS * W * j + q], wp[:, HALF * hf:HALF * (hf + 1)],
                                  start=i_part == 0, stop=i_part == 1)
                last.then_inc(full_sem, 1)

            def y_distances(m, j):
                l, p = where(m)
                r0, r1 = wide(j)
                pe.wait_ge(half_here, 16)
                pe.wait_ge(pos_here, 16)
                pe.wait_ge(pos_ready, 2 * (m + 1))
                full_sem = take(("y", m, j))
                for bb in range(2):
                    last = mm(tbuf(("y", m, j))[0:YROWS, BANK * bb:BANK * bb + (r1 - r0) * W], ey[0:KPOS, j, :],
                              pos[0:KPOS, 2 * p + bb, W * r0:W * r1], start=True, stop=True)
                last.then_inc(full_sem, 1)

            def mask_rows(m, j):
                l, p = where(m)
                r0, r1 = wide(j)
                pe.wait_ge(msk_ready, 2 * (m - PAIRS + 1))
                full_sem = take(("mask", m, j))
                for bb in range(2):
                    last = mm(tbuf(("mask", m, j))[0:YROWS, BANK * bb:BANK * bb + (r1 - r0) * W], my[0:KMASK, 0, :],
                              msk[:, 2 * p + bb, W * r0:W * r1], start=True, stop=True)
                last.then_inc(full_sem, 1)

            def largest_offset(m, _):
                name = ("flag", m, 0)
                pe.wait_ge(omax_ready, 3 * (m + 1))
                full_sem = take(name)
                nc.tensor.transpose(tbuf(name)[0:1, 0:NOFF], omax1[0:NOFF, m:m + 1], ident[0:NOFF, 0:NOFF])\
                    .then_inc(full_sem, 1)

            def x_distances(m, a):
                l, p = where(m)
                k, bb = a
                name = ("tx", m, a)
                if a == (0, 0):
                    pe.wait_ge(pos_ready, 2 * (m + 1))
                full_sem = take(name)
                for hf in range(2):
                    last = mm(tbuf(name)[0:ROWS * W, BANK * hf:BANK * hf + HALF], ex[0:KPOS, k, :],
                              pos[0:KPOS, 2 * p + bb, HALF * hf:HALF * (hf + 1)], start=True, stop=True)
                last.then_inc(full_sem, 1)

            def spread_rows(m, g):
                l, p = where(m)
                k, j = STEPS[g]
                r0, r1 = band(j, k // 3)
                nb = W * (r1 - r0)
                at = WIDE_AT[j] + W * (r0 - wide(j)[0])
                n = NSTEPS * m + g
                pe.wait_ge(ytent_ready, CHUNKS * m + j + 1)
                if n >= ITEM_BUFS:
                    pe.wait_ge(s_ready, n - ITEM_BUFS + 1)
                for bb in range(2):
                    last = mm(ib[0:pixels(j), n % ITEM_BUFS, nb * bb:nb * (bb + 1)], sel[0:YROWS, k, 0:pixels(j)],
                              ytent[:, 2 * p + bb, at:at + nb], start=True, stop=True)
                last.then_inc(item_full[n % ITEM_BUFS], 1)

            def clear_acc():
                for hf in range(2):
                    mm(acc[:, hf, 0:HALF], zeros[0:1, 0:128], zeros[0:1, 0:HALF], start=True, stop=False,
                       skip_group_check=True)

            def products(m, g):
                l, p = where(m)
                k, j = STEPS[g]
                q = pixels(j)
                r0, r1 = band(j, k // 3)
                n = NSTEPS * m + g
                if g == 0:
                    pe.wait_ge(cleared, 4)
                    if m:
                        pe.wait_ge(acc_free, m)
                    clear_acc()
                if k == 0:
                    for bb in range(2):
                        pe.wait_ge(z_ready[bb], CHUNKS * m + j + 1)
                pe.wait_ge(s_ready, n + 1)
                for hf in range(2):
                    a, b = max(r0, 12 * hf), min(r1, 12 * hf + 12)
                    if a >= b:
                        continue
                    for bb in range(2):
                        last = mm(acc[64 * bb:64 * bb + 64, hf, W * (a - 12 * hf):W * (b - 12 * hf)],
                                  z[0:q, 2 * p + bb, j, 64 * k:64 * k + 64],
                                  s[0:q, n % S_SLOTS, bb, W * (a - r0):W * (b - r0)],
                                  start=False, stop=g == NSTEPS - 1, skip_group_check=True)
                last.then_inc(s_used, 1)
                if g == NSTEPS - 1:
                    pe.wait_ge(s_used, NSTEPS * (m + 1))
                    pe.sem_inc(acc_full, 1)

            def general(m):
                l, p = where(m)
                na, nd, np_ = g_steps(l)
                pe.wait_ge(y_ready, m + 1)
                for i in range(JOB_BUFS):
                    pe.wait_ge(t_free[i], (JOBS_BY[m] - 1 - i) // JOB_BUFS + 1)
                pe.wait_ge(s_ready, NSTEPS * (m + 1) + (AHEAD if m + 1 < STAGES else 0))
                clear_acc()
                pe.sem_inc(g_pe[m], 1)
                with pe.Fori(0, TAPS) as k:
                    for bb in range(2):
                        it = 2 * k + bb
                        pe.wait_ge(g_act[m], na * it + 5 + 2 * l)
                        for hf in range(2):
                            last = mm(tb[0:ROWS * W, 0, BANK * hf:BANK * hf + HALF], g_ex,
                                      g_pos[:, HALF * hf:HALF * (hf + 1)], start=True, stop=True)
                        last.then_inc(g_pe[m], 1)
                        for j in range(CHUNKS):
                            q = pixels(j)
                            pe.wait_ge(g_dve[m], nd * it + (2 + l) * j + 1)
                            for hf in range(2):
                                c = slice(HALF * hf, HALF * (hf + 1))
                                last = mm(tb[0:ROWS * W, 1, BANK * hf:BANK * hf + HALF], g_ef,
                                          g_pos[:, c], start=True, stop=True)
                                if l:
                                    last = mm(ib[0:ROWS * W, hf, 0:HALF], g_em,
                                              g_msk[:, c], start=True, stop=True)
                            last.then_inc(g_pe[m], 1)
                            pe.wait_ge(g_dve[m], nd * it + (2 + l) * (j + 1) + 1)
                            for hf in range(2):
                                last = mm(acc[64 * bb:64 * bb + 64, hf, 0:HALF], g_z[0:q, C * j:C * (j + 1)],
                                          g_s[0:q, HALF * hf:HALF * (hf + 1)], start=False, stop=False,
                                          skip_group_check=True)
                            last.then_inc(g_pe[m], 1)
                pe.wait_ge(g_pe[m], np_ * 2 * TAPS + 1)
                pe.sem_inc(g_sum[m], 1)
                pe.wait_ge(g_out[m], 1)

            def final_mean(m, _):
                l, p = where(m)
                pe.wait_ge(fin_stats, 2 * p + 1)
                full_sem = take(("final mean", m, 0))
                mm(tbuf(("final mean", m, 0))[:, 0:2], block_m, fin[:, p, 0:2], start=True, stop=True).then_inc(full_sem, 1)

            def final_variance(m, _):
                l, p = where(m)
                pe.wait_ge(fin_stats, 2 * p + 2)
                full_sem = take(("final variance", m, 0))
                mm(tbuf(("final variance", m, 0))[:, 0:1], block_m, fin[:, p, 5:6], start=True, stop=True)\
                    .then_inc(full_sem, 1)

            part = {"weights": weights, "norm": norm, "conv": conv, "z": z_products, "tx": x_distances, "y": y_distances, "mask": mask_rows,
                    "flag": largest_offset, "final mean": final_mean, "final variance": final_variance}
            pe.wait_ge(full_here, 16)
            for name, n, a in before():
                if name in part:
                    part[name](n, a)
            for g in range(AHEAD):
                spread_rows(0, g)
            for m in range(STAGES):
                for g, at in enumerate(during(m)):
                    if (m, g + AHEAD) in NEXT:
                        spread_rows(*NEXT[m, g + AHEAD])
                    for name, n, a in at:
                        if name in part:
                            part[name](n, a)
                    products(m, g)
                with pe.If(far(pe, m)):
                    general(m)
            final_mean(STAGES - 1, 0)
            final_variance(STAGES - 1, 0)


def kernel(x, L0_conv_w_off, L0_conv_b_off, L0_conv_w_def, L0_conv_b_def,
           L1_conv_w_off, L1_conv_b_off, L1_conv_w, L1_conv_b, L1_conv_gamma, L1_conv_beta):
    import concourse.bacc as bacc
    from concourse.bass_utils import run_bass_kernel_spmd

    def off_rows(a):
        a = np.asarray(a)
        return np.tile(np.pad(a, [(0, 32 - a.shape[0])] + [(0, 0)] * (a.ndim - 1)), [4] + [1] * (a.ndim - 1))

    def taps(w):
        w = np.asarray(w)
        return w.transpose(0, 2, 3, 1).reshape(w.shape[0], TAPS * C)

    def twice(a):
        a = np.asarray(a)
        return np.concatenate([a, a], 0)

    half, full, pos = constants()
    vecs = np.stack([off_rows(L0_conv_b_off), off_rows(L1_conv_b_off), twice(L0_conv_b_def), twice(L1_conv_b),
                     twice(L1_conv_gamma), twice(L1_conv_beta)], 1)
    arrays = {
        "x": np.ascontiguousarray(np.asarray(x).reshape(B, C, HW)),
        "w_off": np.ascontiguousarray(np.stack([off_rows(taps(L0_conv_w_off)), off_rows(taps(L1_conv_w_off))])),
        "w_def": np.ascontiguousarray(np.stack([twice(taps(L0_conv_w_def)), twice(taps(L1_conv_w))])),
        "vecs": np.ascontiguousarray(vecs), "c_half": half, "c_full": full, "c_pos": np.ascontiguousarray(pos),
    }
    nc = bacc.Bacc("TRN2", target_bir_lowering=False, num_devices=1)
    args = {n: nc.dram_tensor(n, a.shape, mybir.dt.from_np(a.dtype), kind="ExternalInput").ap() for n, a in arrays.items()}
    out = nc.dram_tensor("out", (B, C, HW), F32, kind="ExternalOutput").ap()
    build(nc, out=out, **args)
    r = run_bass_kernel_spmd(nc, [arrays], core_ids=[0])
    return r.results[0]["out"].reshape(B, C, H, W)
```
